# Optimizing a Trainium2 kernel written in Bass

```python
import numpy as np
import jax
import jax.numpy as jnp

def _softmax(x, axis=-1):
    return jax.nn.softmax(x, axis=axis)

def _gelu(x):
    return jax.nn.gelu(x, approximate=True)

def _silu(x):
    return jax.nn.silu(x)

def _sigmoid(x):
    return jax.nn.sigmoid(x)

def _layernorm(x, axis=-1, eps=1e-05):
    m = jnp.mean(x, axis=axis, keepdims=True)
    v = jnp.var(x, axis=axis, keepdims=True)
    return (x - m) / jnp.sqrt(v + eps)

def _scatter_add(tgt, idx, src, axis=0):
    return tgt.at[idx].add(src)

def _segment_sum(src, seg, n):
    return jax.ops.segment_sum(src, seg, n)
kernel_name = 'mk_seq_postln_d1_jaxref_r4_5a2d15'

def setup_inputs(seed: int=0):
    np.random.seed(seed)
    _w = jnp.asarray

    def _L0_attn_setup():
        import jax, jax.numpy as jnp
        import numpy as np
        DIM = 256
        HEADS = 16
        HEAD_DIM = DIM // HEADS
        B, N = (2, 512)
        SCALE = 1.0 / np.float32(np.sqrt(DIM))

        def _split_heads(t):
            b, n, _ = t.shape
            return jnp.moveaxis(t.reshape(b, n, HEADS, HEAD_DIM), 2, 0)
        key = jax.random.key(seed)
        ks = jax.random.split(key, 9)
        s = 0.02
        return {'x': jax.random.normal(ks[0], (B, N, DIM), dtype=jnp.float32), 'Wq': jax.random.normal(ks[1], (DIM, DIM), dtype=jnp.float32) * s, 'bq': jax.random.normal(ks[2], (DIM,), dtype=jnp.float32) * s, 'Wk': jax.random.normal(ks[3], (DIM, DIM), dtype=jnp.float32) * s, 'bk': jax.random.normal(ks[4], (DIM,), dtype=jnp.float32) * s, 'Wv': jax.random.normal(ks[5], (DIM, DIM), dtype=jnp.float32) * s, 'bv': jax.random.normal(ks[6], (DIM,), dtype=jnp.float32) * s, 'Wo': jax.random.normal(ks[7], (DIM, DIM), dtype=jnp.float32) * s, 'bo': jax.random.normal(ks[8], (DIM,), dtype=jnp.float32) * s}
    _L0_attn_in = _L0_attn_setup()

    def _L0_ffn_setup():
        import jax, jax.numpy as jnp
        import numpy as np
        DIM = 256
        HIDDEN = 768
        SCALE = 1.0 / 127.0

        def _dequant(w_int, dtype):
            return w_int.astype(dtype) * jnp.asarray(SCALE, dtype)
        key = jax.random.key(seed)
        k_x, k_g, k_u, k_d = jax.random.split(key, 4)
        x = jax.random.normal(k_x, (4, 512, DIM), dtype=jnp.float32)
        w_gate = jax.random.randint(k_g, (HIDDEN, DIM), -127, 128, dtype=jnp.int32)
        w_up = jax.random.randint(k_u, (HIDDEN, DIM), -127, 128, dtype=jnp.int32)
        w_down = jax.random.randint(k_d, (DIM, HIDDEN), -127, 128, dtype=jnp.int32)
        return {'x': x, 'w_gate': w_gate, 'w_up': w_up, 'w_down': w_down}
    _L0_ffn_in = _L0_ffn_setup()
    _d = {'L0_attn_x': _L0_attn_in['x'], 'L0_attn_Wq': _L0_attn_in['Wq'], 'L0_attn_bq': _L0_attn_in['bq'], 'L0_attn_Wk': _L0_attn_in['Wk'], 'L0_attn_bk': _L0_attn_in['bk'], 'L0_attn_Wv': _L0_attn_in['Wv'], 'L0_attn_bv': _L0_attn_in['bv'], 'L0_attn_Wo': _L0_attn_in['Wo'], 'L0_attn_bo': _L0_attn_in['bo'], 'L0_ffn_w_gate': _L0_ffn_in['w_gate'], 'L0_ffn_w_up': _L0_ffn_in['w_up'], 'L0_ffn_w_down': _L0_ffn_in['w_down']}
    _x0 = _d['L0_attn_x']
    _d['L0_attn_x'] = jax.random.normal(jax.random.fold_in(jax.random.key(seed), 1), (16, 1024, 256), dtype=_x0.dtype)
    del _x0
    return _d

def reference(L0_attn_x, L0_attn_Wq, L0_attn_bq, L0_attn_Wk, L0_attn_bk, L0_attn_Wv, L0_attn_bv, L0_attn_Wo, L0_attn_bo, L0_ffn_w_gate, L0_ffn_w_up, L0_ffn_w_down):

    def _L0_attn_ref(x, Wq, bq, Wk, bk, Wv, bv, Wo, bo):
        import jax, jax.numpy as jnp
        import numpy as np
        DIM = 256
        HEADS = 16
        HEAD_DIM = DIM // HEADS
        B, N = (2, 512)
        SCALE = 1.0 / np.float32(np.sqrt(DIM))

        def _split_heads(t):
            b, n, _ = t.shape
            return jnp.moveaxis(t.reshape(b, n, HEADS, HEAD_DIM), 2, 0)
        q = _split_heads(x @ Wq.T + bq)
        k = _split_heads(x @ Wk.T + bk)
        v = _split_heads(x @ Wv.T + bv)
        scores = jnp.einsum('hbnd,hbmd->hbnm', k, q) * SCALE
        attn = jax.nn.softmax(scores, axis=-1)
        out = jnp.einsum('hbnm,hbmd->hbnd', attn, v)
        out = jnp.moveaxis(out, 0, 2).reshape(x.shape[0], x.shape[1], DIM)
        return out @ Wo.T + bo

    def _L0_ffn_ref(x, w_gate, w_up, w_down):
        import jax, jax.numpy as jnp
        import numpy as np
        DIM = 256
        HIDDEN = 768
        SCALE = 1.0 / 127.0

        def _dequant(w_int, dtype):
            return w_int.astype(dtype) * jnp.asarray(SCALE, dtype)
        wg = _dequant(w_gate, x.dtype)
        wu = _dequant(w_up, x.dtype)
        wd = _dequant(w_down, x.dtype)
        gate = jnp.einsum('bsd,hd->bsh', x, wg)
        up = jnp.einsum('bsd,hd->bsh', x, wu)
        h = jax.nn.silu(gate) * up
        return jnp.einsum('bsh,dh->bsd', h, wd)
    x = L0_attn_x
    x = _layernorm(x + _L0_attn_ref(x, L0_attn_Wq, L0_attn_bq, L0_attn_Wk, L0_attn_bk, L0_attn_Wv, L0_attn_bv, L0_attn_Wo, L0_attn_bo), axis=-1)
    x = _layernorm(x + _L0_ffn_ref(x, L0_ffn_w_gate, L0_ffn_w_up, L0_ffn_w_down), axis=-1)
    return x

_drawn_inputs = setup_inputs


def setup_inputs(seed=0):
    import zlib

    import numpy as np

    out = dict(_drawn_inputs(seed))
    spreads = {}
    factors = {'L0_attn_Wq': 8.0,
     'L0_attn_bq': 8.0,
     'L0_attn_Wk': 8.0,
     'L0_attn_bk': 8.0,
     'L0_attn_Wv': 8.0,
     'L0_attn_bv': 6.011,
     'L0_attn_Wo': 5.493}
    for name, (base, spread) in spreads.items():
        noise = np.random.default_rng([zlib.crc32(name.encode()), seed]).standard_normal(out[name].shape)
        drawn = base * np.exp(spread * noise) if base else spread * noise
        out[name] = jnp.asarray(drawn.astype(out[name].dtype))
    for name, factor in factors.items():
        out[name] = (out[name] * factor).astype(out[name].dtype)
    return out
```

```python
from contextlib import ExitStack

import concourse.bass as bass
from concourse import mybir

F32 = mybir.dt.float32
BF16 = mybir.dt.bfloat16
I32 = mybir.dt.int32
ALU = mybir.AluOpType
ACT = mybir.ActivationFunctionType
AX_X = mybir.AxisListType.X
RMAX = bass.bass_isa.ReduceOp.max

P = 128
BATCHES = 16
TOKENS = 1024
DIM = 256
HIDDEN = 768
HEADS = 16
HEAD_DIM = DIM // HEADS
TILES = TOKENS // P
CHUNKS = DIM // P
HCHUNKS = HIDDEN // P
HALF = 512
HALVES = TOKENS // HALF
TPH = TILES // HALVES
GROUP = 4
GROUPS = HEADS // GROUP
CHEADS = P // HEAD_DIM
VW = 32
EPS = 1e-5
SCORE_SCALE = 1.0 / 16.0
SCORE_BOUND = 40.0
NORM_MARGIN = 1.02
NORM_LIMIT = (SCORE_BOUND / SCORE_SCALE) ** 2
W_SCALE = 1.0 / 127.0

Q_PARTS = (0, 0, 0, 1, 1, 2)
K_PARTS = (0, 1, 2, 0, 1, 0)
ROWS = len(Q_PARTS) * HEAD_DIM
SHIFT_ROWS = 3

PRE = 16
QK0 = 4
V0 = 12
QK = 8
UNITS = HEADS * TILES
STEPS = GROUPS * TILES
NORMS = 8
POST = 40
O0, X0, G0, D0 = 4, 8, 12, 36
LOADS = 4 * len(Q_PARTS)
GEN_FILL = UNITS + 1
GEN_FREE = UNITS + 2


def build(nc, x, Wq, bq, Wk, bk, Wv, bv, Wo, bo, w_gate, w_up, w_down, out):
    ctx = ExitStack()
    with ctx:
        def sb(name, shape, dt=F32):
            return ctx.enter_context(nc.sbuf_tensor(name, shape, dt))

        def sem(name):
            return ctx.enter_context(nc.semaphore(name))

        qstack = sb("qstack", [ROWS + SHIFT_ROWS, HEADS, TOKENS], BF16)
        kstack = sb("kstack", [ROWS + SHIFT_ROWS, HEADS, TOKENS], BF16)
        probs = sb("probs", [P, 2, GROUP, TOKENS])
        v = sb("v", [P, TILES, HEADS, VW])
        x_pre = sb("x_pre", [P, TILES, DIM])
        x_res = sb("x_res", [P, TILES, DIM])
        xT = sb("xT", [P, CHUNKS, TOKENS])
        parts = sb("parts", [P, 2, 3, TOKENS], BF16)
        rest = sb("rest", [P, 2, HALF])
        squares = sb("squares", [P, 4, TOKENS], BF16)
        accT = sb("accT", [P, TOKENS])
        attn = sb("attn", [P, TILES, DIM])
        WqT = sb("WqT", [P, CHUNKS, DIM])
        WkT = sb("WkT", [P, CHUNKS, DIM])
        WvT = sb("WvT", [P, CHUNKS, DIM])
        WoT = sb("WoT", [P, CHUNKS, DIM])
        gateT = sb("gateT", [P, CHUNKS, HIDDEN])
        upT = sb("upT", [P, CHUNKS, HIDDEN])
        downT = sb("downT", [P, HCHUNKS, DIM])
        bqk = sb("bqk", [P, 4])
        bv_all = sb("bv_all", [P, DIM])
        bo_all = sb("bo_all", [P, DIM])
        ident = sb("ident", [P, P])
        blocks = sb("blocks", [P, P], BF16)
        norms = sb("norms", [P, NORMS])
        norm2 = sb("norm2", [P, 2])
        norm2_safe = sb("norm2_safe", [P, 2])
        norm2_all = sb("norm2_all", [P, 2])
        flag = sb("flag", [P, 1], I32)
        rowmax = sb("rowmax", [P, UNITS])
        shift = sb("shift", [P, 2, P])
        shift_parts = sb("shift_parts", [P, SHIFT_ROWS, P], BF16)
        inv = sb("inv", [P, HALVES, TPH, GROUP])
        stats = sb("stats", [P, TILES, 6])
        meanvar = sb("meanvar", [P, TILES, 2])
        vareps = sb("vareps", [P, TILES])
        rstd = sb("rstd", [P, TILES])
        minus_half = sb("minus_half", [P, TILES])
        eps = sb("eps", [P, TILES])
        margin = sb("margin", [P, 2])

        flat = probs[:, :, :, :].rearrange("p a g n -> p (a g n)")
        attnT = flat[:, 0:CHUNKS * TOKENS].rearrange("p (c n) -> p c n", c=CHUNKS)
        H = HCHUNKS * HALF
        hT = [flat[:, s * H:(s + 1) * H].rearrange("p (c n) -> p c n", c=HCHUNKS) for s in range(HALVES)]
        tanh_out = [flat[:, 2 * H + s * HALF:2 * H + (s + 1) * HALF] for s in range(2)]
        gated = [flat[:, 2 * H + (2 + s) * HALF:2 * H + (3 + s) * HALF] for s in range(2)]
        w4_raw = flat[:, 0:2048].rearrange("p (w c n) -> p w c n", w=4, c=CHUNKS)
        ints = flat[:, 2048:2048 + 3 * 1536]
        gate_raw = flat[:, 2048:3584].rearrange("p (c n) -> p c n", c=HCHUNKS)
        up_raw = flat[:, 3584:5120].rearrange("p (c n) -> p c n", c=HCHUNKS)
        down_raw = flat[:, 5120:6656].rearrange("p (c n) -> p c n", c=CHUNKS)

        psum = ctx.enter_context(nc.psum_tensor("psum", [P, 8, HALF], F32))
        bank = [psum[:, i, :] for i in range(8)]
        scores = [psum[:, 2 * s:2 * s + 2, :] for s in range(2)]
        ACC, TR = 4, 6

        parts_dram = nc.dram_tensor("parts_dram", (4, 3, P, TOKENS), BF16, kind="Internal").ap()

        weights_loaded = sem("weights_loaded")
        biases_loaded = sem("biases_loaded")
        ints_float = sem("ints_float")
        consts_ready = sem("consts_ready")
        pool_step = sem("pool_step")
        setup_fill, setup_free = sem("setup_fill"), sem("setup_free")
        x_pre_loaded, x_res_loaded, x_res_biased = sem("x_pre_loaded"), sem("x_res_loaded"), sem("x_res_biased")
        pre_fill, pre_free = sem("pre_fill"), sem("pre_free")
        hi_ready, mid_ready, lo_ready, squares_ready = sem("hi_ready"), sem("mid_ready"), sem("lo_ready"), sem("squares_ready")
        parts_stored = [sem("parts_stored0"), sem("parts_stored1")]
        stacks_loaded = sem("stacks_loaded")
        norm_fill, norm_free = sem("norm_fill"), sem("norm_free")
        norm2_ready, norm2_reduced, flag_ready = sem("norm2_ready"), sem("norm2_reduced"), sem("flag_ready")
        gen_fill, gen_free = sem("gen_fill"), sem("gen_free")
        shift_ready, shift_loaded = sem("shift_ready"), sem("shift_loaded")
        scores_ready, probs_ready, pv_done = sem("scores_ready"), sem("probs_ready"), sem("pv_done")
        acc_copied = sem("acc_copied")
        tr_fill, tr_free = sem("tr_fill"), sem("tr_free")
        post_fill, post_free = sem("post_fill"), sem("post_free")
        tanh_ready = sem("tanh_ready")
        stats_ready, rstd_ready, x1_ready, y_ready = sem("stats_ready"), sem("rstd_ready"), sem("x1_ready"), sem("y_ready")
        out_stored = sem("out_stored")
        dve_step = sem("dve_step")

        x_v = x.rearrange("b (p t) d -> b p t d", t=TILES)
        out_v = out.rearrange("b (p t) d -> b p t d", t=TILES)

        block = ctx.enter_context(nc.Block())

        @block.sync
        def _(sp):
            for n, w in enumerate((Wq, Wk, Wv, Wo)):
                sp.dma_start(w4_raw[:, n, :, :], w.rearrange("(c p) k -> p c k", p=P)).then_inc(weights_loaded, 16)
            for dst, w in ((gate_raw, w_gate), (up_raw, w_up), (down_raw, w_down)):
                sp.dma_start(dst.bitcast(I32), w.rearrange("(c p) k -> p c k", p=P)).then_inc(weights_loaded, 16)
            with nc.allow_non_contiguous_dma(reason="two bias vectors, once"):
                sp.dma_start(bqk[:, 0:2], bq.rearrange("(c p) -> p c", p=P)).then_inc(biases_loaded, 16)
                sp.dma_start(bqk[:, 2:4], bk.rearrange("(c p) -> p c", p=P)).then_inc(biases_loaded, 16)
            sp.dma_start(bv_all[:, :], bv.partition_broadcast(P)).then_inc(biases_loaded, 16)
            sp.dma_start(bo_all[:, :], bo.partition_broadcast(P)).then_inc(biases_loaded, 16)

            def load_x_pre(b):
                sp.dma_start(x_pre[:, :, :], x_v[b]).then_inc(x_pre_loaded, 16)

            def restack(b, first):
                def load(idx):
                    t, c = idx // 2, idx % 2
                    sp.wait_ge(parts_stored[idx % 2], 32 * b + 16 * (idx // 2 + 1))
                    stack, which = ((qstack, Q_PARTS), (kstack, K_PARTS))[t]
                    for r, part in enumerate(which):
                        sp.dma_start(stack[r * HEAD_DIM:(r + 1) * HEAD_DIM, c * CHEADS:(c + 1) * CHEADS, :],
                                     parts_dram[idx, part].rearrange("(h d) n -> d h n", d=HEAD_DIM)
                                     ).then_inc(stacks_loaded, 16)

                for idx in range(4):
                    sp.wait_ge(lo_ready, QK * b + 2 * idx + 2)
                    sp.wait_ge(squares_ready, QK * b + 2 * idx + 2)
                    sp.dma_start(parts_dram[idx].rearrange("j p n -> p j n"), parts[:, idx % 2, :, :]
                                 ).then_inc(parts_stored[idx % 2], 16)
                    if idx == 1 and not first:
                        sp.wait_ge(scores_ready, UNITS * b)
                    if idx >= 1:
                        load(idx - 1)
                load(3)
                sp.wait_ge(stacks_loaded, 16 * LOADS * (b + 1))

            def load_shift(b):
                sp.wait_ge(shift_ready, b + 1)
                for r in range(SHIFT_ROWS):
                    sp.dma_start(kstack[ROWS + r:ROWS + r + 1, :, :].rearrange("o h (t n) -> o (h t) n", t=TILES),
                                 shift_parts[:, r, :]).then_inc(shift_loaded, 16)

            def store_out(b):
                for s in range(2):
                    sp.wait_ge(y_ready, 4 * b + 2 * (s + 1))
                    sp.dma_start(out_v[b][:, 4 * s:4 * s + 4, :], x_res[:, 4 * s:4 * s + 4, :]).then_inc(out_stored, 16)

            def load_x_res(b, first):
                if not first:
                    sp.wait_ge(out_stored, 32 * b)
                sp.dma_start(x_res[:, :, :], x_v[b]).then_inc(x_res_loaded, 16)

            load_x_pre(0)
            restack(0, True)

            def batch(b, first, last):
                load_x_res(b, first)
                if not last:
                    sp.wait_ge(pre_fill, PRE * b + QK0)
                    load_x_pre(b + 1)
                load_shift(b)
                if not last:
                    restack(b + 1, False)
                store_out(b)

            batch(0, True, False)
            with sp.Fori(1, BATCHES - 1) as b:
                batch(b, False, False)
            batch(BATCHES - 1, False, True)
            sp.wait_ge(out_stored, 32 * BATCHES)

        @block.gpsimd
        def _(pool):
            step = 0

            def then(ins):
                nonlocal step
                step += 1
                ins.then_inc(pool_step, 1)
                pool.wait_ge(pool_step, step)

            then(nc.gpsimd.memset(ident[:, :], 0.0))
            nc.gpsimd.affine_select(out=ident[:, :], in_=ident[:, :], compare_op=ALU.not_equal, fill=1.0, base=0,
                                    pattern=[[-1, P]], channel_multiplier=1).then_inc(consts_ready, 1)
            then(nc.gpsimd.memset(blocks[:, :], 1.0))
            blk = blocks[:, :].rearrange("p (h d) -> p h d", d=HEAD_DIM)
            then(nc.gpsimd.affine_select(out=blk, in_=blk, compare_op=ALU.is_ge, fill=0.0, base=0,
                                         pattern=[[-HEAD_DIM, CHEADS], [0, HEAD_DIM]], channel_multiplier=1))
            nc.gpsimd.affine_select(out=blk, in_=blk, compare_op=ALU.is_ge, fill=0.0, base=HEAD_DIM - 1,
                                    pattern=[[HEAD_DIM, CHEADS], [0, HEAD_DIM]], channel_multiplier=-1
                                    ).then_inc(consts_ready, 1)
            then(nc.gpsimd.memset(v[:, :, :, :], 0.0))
            nc.gpsimd.memset(v[:, :, :, HEAD_DIM:HEAD_DIM + 1], 1.0).then_inc(consts_ready, 1)
            then(nc.gpsimd.memset(minus_half[:, :], -0.5))
            then(nc.gpsimd.memset(eps[:, :], EPS))
            then(nc.gpsimd.memset(margin[:, :], NORM_MARGIN))
            setup_steps = step

            def pre(b, first):
                for j in range(QK):
                    s, idx, hf = j % 2, j // 2, j % 2
                    cols = slice(hf * HALF, (hf + 1) * HALF)
                    pool.wait_ge(mid_ready, QK * b + j + 1)
                    nc.gpsimd.tensor_tensor(parts[:, idx % 2, 2, cols], rest[:, s, :], parts[:, idx % 2, 1, cols],
                                            ALU.subtract).then_inc(lo_ready, 1)
                    if j == 0 and not first:
                        pool.wait_ge(norm_free, NORMS * b)
                    nc.gpsimd.tensor_tensor(squares[:, idx, cols], parts[:, idx % 2, 0, cols],
                                            parts[:, idx % 2, 0, cols], ALU.mult).then_inc(squares_ready, 1)

            def bound(b):
                pool.wait_ge(norm2_ready, b + 1)
                nc.gpsimd.tensor_tensor(norm2_safe[:, :], norm2[:, :], margin[:, :], ALU.mult)
                pool.drain()
                nc.gpsimd.partition_all_reduce(norm2_all[:, :], norm2_safe[:, :], P, RMAX).then_inc(norm2_reduced, 1)

            def make_rstd(b, j, which):
                tiles = slice(2 * j, 2 * j + 2)
                n = TILES * b + 4 * which + j
                pool.wait_ge(stats_ready, n + 1)
                nc.gpsimd.tensor_tensor(vareps[:, tiles], meanvar[:, tiles, 1], eps[:, tiles], ALU.add
                                        ).then_inc(pool_step, 1)
                pool.wait_ge(pool_step, n + 1 + setup_steps)
                nc.gpsimd.tensor_tensor(rstd[:, tiles], vareps[:, tiles], minus_half[:, tiles], ALU.pow
                                        ).then_inc(rstd_ready, 1)

            def batch(b, last):
                pool.wait_ge(x_res_loaded, 16 * (b + 1))
                nc.gpsimd.tensor_tensor(x_res[:, :, :], x_res[:, :, :],
                                        bo_all[:, :].unsqueeze(1).to_broadcast([P, TILES, DIM]), ALU.add
                                        ).then_inc(x_res_biased, 1)
                if not last:
                    pre(b + 1, False)
                for j in range(4):
                    make_rstd(b, j, 0)
                if not last:
                    bound(b + 1)
                for j in range(4):
                    make_rstd(b, j, 1)

            pool.wait_ge(biases_loaded, 64)
            pre(0, True)
            bound(0)
            batch(0, False)
            with pool.Fori(1, BATCHES - 1) as b:
                batch(b, False)
            batch(BATCHES - 1, True)

        @block.scalar
        def _(act):
            act.wait_ge(biases_loaded, 64)

            def pre(b, first):
                def hi(j):
                    idx, hf = j // 2, j % 2
                    act.wait_ge(pre_fill, PRE * b + QK0 + j + 1)
                    if hf == 0 and not (first and idx < 2):
                        act.wait_ge(parts_stored[idx % 2], 32 * b + 16 * (idx // 2))
                    nc.scalar.activation(parts[:, idx % 2, 0, hf * HALF:(hf + 1) * HALF], bank[(QK0 + j) % 4],
                                         ACT.Identity, bias=bqk[:, idx:idx + 1]).then_inc(hi_ready, 1)

                def mid(j):
                    idx, hf = j // 2, j % 2
                    act.wait_ge(pre_free, PRE * b + QK0 + j + 1)
                    nc.scalar.activation(parts[:, idx % 2, 1, hf * HALF:(hf + 1) * HALF], rest[:, j % 2, :],
                                         ACT.Copy).then_inc(mid_ready, 1)

                for j in range(QK + 1):
                    if j < QK:
                        hi(j)
                    if j >= 1:
                        mid(j - 1)

            def attention(b, first):
                if not first:
                    act.wait_ge(post_free, POST * b)
                for u in range(UNITS):
                    k, h = u // GROUP, u % GROUP
                    act.wait_ge(scores_ready, UNITS * b + u + 1)
                    if h == 0 and k >= 2:
                        act.wait_ge(pv_done, 2 * STEPS * b + 2 * (k - 1))
                    nc.scalar.activation(probs[:, k % 2, h, :], scores[u % 2].rearrange("p a n -> p (a n)"), ACT.Exp,
                                         scale=SCORE_SCALE).then_inc(probs_ready, 1)

            def post(b):
                for g in range(2 * HCHUNKS):
                    act.wait_ge(post_fill, POST * b + G0 + 2 * g + 1)
                    if g >= 2:
                        act.wait_ge(post_free, POST * b + G0 + 2 * (g - 2) + 1)
                    nc.scalar.activation(tanh_out[g % 2], bank[(G0 + 2 * g) % 4], ACT.Tanh, scale=0.5 * W_SCALE
                                         ).then_inc(tanh_ready, 1)

            pre(0, True)

            def batch(b, first, last):
                attention(b, first)
                if not last:
                    pre(b + 1, False)
                post(b)

            batch(0, True, False)
            with act.Fori(1, BATCHES - 1) as b:
                batch(b, False, False)
            batch(BATCHES - 1, False, True)

        @block.vector
        def _(dve):
            nc.vector.memset(qstack[ROWS:ROWS + SHIFT_ROWS, :, :], 1.0).then_inc(consts_ready, 1)
            dve.wait_ge(weights_loaded, 16 * 7)
            nc.vector.tensor_copy(ints, ints.bitcast(I32)).then_inc(ints_float, 1)
            targets = [WqT, WkT, WvT, WoT]
            views = [t[:, :, :].rearrange("p c n -> p (c n)") for t in targets]
            for t in (gateT, upT, downT):
                w = t[:, :, :].rearrange("p c n -> p (c n)")
                views += [w[:, i * HALF:(i + 1) * HALF] for i in range(3)]
            for f, w in enumerate(views):
                dve.wait_ge(setup_fill, f + 1)
                nc.vector.tensor_copy(w, bank[f % 4]).then_inc(setup_free, 1)
            dve.wait_ge(biases_loaded, 64)

            def pre(b, first):
                for f in range(4):
                    hf, c = f // 2, f % 2
                    dve.wait_ge(pre_fill, PRE * b + f + 1)
                    nc.vector.tensor_copy(xT[:, c, hf * HALF:(hf + 1) * HALF], bank[f % 4]).then_inc(pre_free, 1)
                for j in range(QK):
                    idx, hf = j // 2, j % 2
                    dve.wait_ge(hi_ready, QK * b + j + 1)
                    if j >= 2 or not first:
                        dve.wait_ge(lo_ready, QK * b + j - 1)
                    nc.vector.scalar_tensor_tensor(out=rest[:, j % 2, :], in0=bank[(QK0 + j) % 4],
                                                   scalar=bqk[:, idx:idx + 1],
                                                   in1=parts[:, idx % 2, 0, hf * HALF:(hf + 1) * HALF],
                                                   op0=ALU.add, op1=ALU.subtract).then_inc(pre_free, 1)
                if first:
                    dve.wait_ge(consts_ready, 4)
                for f in range(4):
                    dve.wait_ge(pre_fill, PRE * b + V0 + f + 1)
                    for i in range(2):
                        ins = nc.vector.tensor_tensor(
                            v[:, 2 * f + i, :, 0:HEAD_DIM],
                            bank[(V0 + f) % 4][:, i * DIM:(i + 1) * DIM].rearrange("p (h d) -> p h d", d=HEAD_DIM),
                            bv_all[:, :].rearrange("p (h d) -> p h d", d=HEAD_DIM), ALU.add)
                    ins.then_inc(pre_free, 1)

            def bound(b):
                for j in range(NORMS):
                    dve.wait_ge(norm_fill, NORMS * b + j + 1)
                    nc.vector.tensor_reduce(norms[:, j:j + 1], bank[ACC + j % 2], AX_X, ALU.max).then_inc(norm_free, 1)
                dve.wait_ge(norm_free, NORMS * (b + 1))
                nc.vector.tensor_reduce(norm2[:, :], norms[:, :].rearrange("p (t j) -> p t j", t=2), AX_X, ALU.max
                                        ).then_inc(norm2_ready, 1)

            def decide(b):
                dve.wait_ge(norm2_reduced, b + 1)
                nc.vector.tensor_scalar(flag[:, :], norm2_all[:, 0:1], norm2_all[:, 1:2], NORM_LIMIT, ALU.mult,
                                        ALU.is_ge).then_inc(flag_ready, 1)

            def attention(b, first):
                if first:
                    dve.wait_ge(flag_ready, 1)
                general = dve.value_load(flag[0:1, 0:1], min_val=0, max_val=1)
                with dve.If(general == 1):
                    dve.sem_inc(gen_free, 2)
                    with dve.Fori(0, HEADS) as h:
                        for t in range(TILES):
                            dve.wait_ge(gen_fill, GEN_FILL * b + TILES * h + t + 1)
                            nc.vector.tensor_reduce(rowmax[:, bass.ds(TILES * h + t, 1)],
                                                    scores[t % 2].rearrange("p a n -> p (a n)"), AX_X, ALU.max
                                                    ).then_inc(gen_free, 1)
                    dve.wait_ge(gen_fill, GEN_FILL * (b + 1))
                    nc.vector.tensor_scalar(shift[:, 0, :], bank[TR][:, 0:P], -1.0, None, ALU.mult)
                    dve.drain()
                    if not first:
                        dve.wait_ge(shift_loaded, 16 * SHIFT_ROWS * b)
                    nc.vector.tensor_copy(shift_parts[:, 0, :], shift[:, 0, :])
                    dve.drain()
                    nc.vector.tensor_tensor(shift[:, 1, :], shift[:, 0, :], shift_parts[:, 0, :], ALU.subtract)
                    dve.drain()
                    nc.vector.tensor_copy(shift_parts[:, 1, :], shift[:, 1, :])
                    dve.drain()
                    nc.vector.tensor_tensor(shift_parts[:, 2, :], shift[:, 1, :], shift_parts[:, 1, :], ALU.subtract
                                            ).then_inc(shift_ready, 1)
                with dve.Else():
                    dve.sem_inc(gen_free, GEN_FREE)
                    if not first:
                        dve.wait_ge(shift_loaded, 16 * SHIFT_ROWS * b)
                    nc.vector.memset(shift_parts[:, :, :], 0.0).then_inc(shift_ready, 1)

            def take_group(b, g):
                for hf in range(HALVES):
                    dve.wait_ge(pv_done, 2 * STEPS * b + 2 * (TILES * (g + 1) - 1) + hf + 1)
                    nc.vector.tensor_copy(accT[:, hf * HALF:(hf + 1) * HALF], bank[ACC + hf]).then_inc(acc_copied, 1)

            def normalise_group(b, g, step):
                for hf in range(HALVES):
                    n = 2 * g + hf
                    dve.wait_ge(tr_fill, 2 * GROUPS * b + n + 1)
                    o = bank[TR + hf].rearrange("p (t h w) -> p t h w", t=TPH, w=VW)
                    nc.vector.reciprocal(inv[:, hf, :, :], o[:, :, :, HEAD_DIM]).then_inc(dve_step, 1)
                    dve.wait_ge(dve_step, step(b))
                    nc.vector.tensor_tensor(
                        attn[:, hf * TPH:(hf + 1) * TPH, g * GROUP * HEAD_DIM:(g + 1) * GROUP * HEAD_DIM].rearrange(
                            "p t (h d) -> p t h d", d=HEAD_DIM),
                        o[:, :, :, 0:HEAD_DIM], inv[:, hf, :, :].unsqueeze(3).to_broadcast([P, TPH, GROUP, HEAD_DIM]),
                        ALU.mult).then_inc(tr_free, 1)

            def add_and_stats(b, f, j, scale, step):
                tiles = x_res[:, 2 * j:2 * j + 2, :].rearrange("p t d -> p (t d)")
                nc.vector.scalar_tensor_tensor(out=tiles, in0=bank[f % 4], scalar=scale, in1=tiles, op0=ALU.mult,
                                               op1=ALU.add).then_inc(post_free, 1)
                dve.wait_ge(post_free, POST * b + f + 1)
                for i in range(2):
                    ins = nc.vector.bn_stats(stats[:, 2 * j + i, :], x_res[:, 2 * j + i, :])
                dve.drain()
                for i in range(2):
                    ins = nc.vector.bn_aggr(meanvar[:, 2 * j + i, :], stats[:, 2 * j + i, :])
                ins.then_inc(stats_ready, 1)

            def normalise(b, j, which, done):
                dve.wait_ge(rstd_ready, TILES * b + 4 * which + j + 1)
                for i in range(2):
                    t = 2 * j + i
                    ins = nc.vector.tensor_scalar(x_res[:, t, :], x_res[:, t, :], meanvar[:, t, 0:1],
                                                  rstd[:, t:t + 1], ALU.subtract, ALU.mult)
                ins.then_inc(done, 1)

            def post(b, last, step):
                normalise_group(b, GROUPS - 1, step)
                for f in range(4):
                    hf, c = f // 2, f % 2
                    dve.wait_ge(post_fill, POST * b + f + 1)
                    nc.vector.tensor_copy(attnT[:, c, hf * HALF:(hf + 1) * HALF], bank[f % 4]).then_inc(post_free, 1)
                dve.wait_ge(x_res_biased, b + 1)
                for j in range(4):
                    dve.wait_ge(post_fill, POST * b + O0 + j + 1)
                    add_and_stats(b, O0 + j, j, 1.0, step)
                    if j >= 1:
                        normalise(b, j - 1, 0, x1_ready)
                normalise(b, 3, 0, x1_ready)
                if not last:
                    bound(b + 1)
                for f in range(4):
                    hf, c = f // 2, f % 2
                    dve.wait_ge(post_fill, POST * b + X0 + f + 1)
                    nc.vector.tensor_copy(xT[:, c, hf * HALF:(hf + 1) * HALF], bank[(X0 + f) % 4]).then_inc(post_free, 1)
                if not last:
                    decide(b + 1)
                for g in range(2 * HCHUNKS):
                    hf, hc, f = g // HCHUNKS, g % HCHUNKS, G0 + 2 * g
                    if g == 2 and not last:
                        dve.wait_ge(flag_ready, b + 2)
                    dve.wait_ge(tanh_ready, 2 * HCHUNKS * b + g + 1)
                    nc.vector.scalar_tensor_tensor(out=gated[g % 2], in0=tanh_out[g % 2], scalar=1.0, in1=bank[f % 4],
                                                   op0=ALU.add, op1=ALU.mult).then_inc(post_free, 1)
                    dve.wait_ge(post_fill, POST * b + f + 2)
                    dve.wait_ge(post_free, POST * b + f + 1)
                    nc.vector.tensor_tensor(hT[hf][:, hc, :], gated[g % 2], bank[(f + 1) % 4], ALU.mult
                                            ).then_inc(post_free, 1)
                for j in range(4):
                    dve.wait_ge(post_fill, POST * b + D0 + j + 1)
                    add_and_stats(b, D0 + j, j, 0.5 * W_SCALE ** 3, step)
                    if j >= 1:
                        normalise(b, j - 1, 1, y_ready)
                normalise(b, 3, 1, y_ready)

            def batch(b, first, last):
                at = [0]

                def step(b):
                    at[0] += 1
                    return DVE_STEPS * b + at[0]

                attention(b, first)
                for g in range(GROUPS):
                    take_group(b, g)
                    if g < GROUPS - 1:
                        normalise_group(b, g, step)
                if not last:
                    pre(b + 1, False)
                post(b, last, step)
                assert at[0] == DVE_STEPS

            DVE_STEPS = 2 * GROUPS

            pre(0, True)
            bound(0)
            decide(0)
            batch(0, True, False)
            with dve.Fori(1, BATCHES - 1) as b:
                batch(b, False, False)
            batch(BATCHES - 1, False, True)

        @block.tensor
        def _(pe):
            def mm(o, lhsT, rhs, start, stop):
                return nc.tensor.matmul(o, lhsT, rhs, start=start, stop=stop)

            def flip(o, src):
                return nc.tensor.transpose(o, src, ident[:, :])

            pe.wait_ge(consts_ready, 4)
            pe.wait_ge(weights_loaded, 16 * 7)
            pe.wait_ge(ints_float, 1)
            tiles = []
            for n in range(4):
                tiles += [w4_raw[:, n, o, k * P:(k + 1) * P] for k in range(CHUNKS) for o in range(CHUNKS)]
            for raw in (gate_raw, up_raw):
                tiles += [raw[:, hc, k * P:(k + 1) * P] for k in range(CHUNKS) for hc in range(HCHUNKS)]
            tiles += [down_raw[:, c, hc * P:(hc + 1) * P] for hc in range(HCHUNKS) for c in range(CHUNKS)]
            fills = len(tiles) // 4
            for f in range(fills):
                if f >= 4:
                    pe.wait_ge(setup_free, f - 3)
                for i in range(4):
                    ins = flip(bank[f % 4][:, i * P:(i + 1) * P], tiles[4 * f + i])
                ins.then_inc(setup_fill, 1)
            pe.wait_ge(setup_free, fills)

            def pre(b, first):
                def slot(f):
                    if f >= 4:
                        pe.wait_ge(pre_free, PRE * b + f - 3)

                if not first:
                    pe.wait_ge(probs_ready, UNITS * b)
                pe.wait_ge(x_pre_loaded, 16 * (b + 1))
                for f in range(4):
                    hf, c = f // 2, f % 2
                    for i in range(TPH):
                        ins = flip(bank[f][:, i * P:(i + 1) * P], x_pre[:, hf * TPH + i, c * P:(c + 1) * P])
                    ins.then_inc(pre_fill, 1)
                pe.wait_ge(pre_free, PRE * b + 4)
                for j in range(QK):
                    idx, hf, f = j // 2, j % 2, QK0 + j
                    w, c = (WqT, WkT)[idx // 2], idx % 2
                    slot(f)
                    for k in range(CHUNKS):
                        ins = mm(bank[f % 4], w[:, k, c * P:(c + 1) * P], xT[:, k, hf * HALF:(hf + 1) * HALF],
                                 k == 0, k == CHUNKS - 1)
                    ins.then_inc(pre_fill, 1)
                for j in range(4):
                    f = V0 + j
                    slot(f)
                    for i in range(2):
                        t = 2 * j + i
                        for k in range(CHUNKS):
                            ins = mm(bank[f % 4][:, i * DIM:(i + 1) * DIM], xT[:, k, t * P:(t + 1) * P], WvT[:, k, :],
                                     k == 0, k == CHUNKS - 1)
                    ins.then_inc(pre_fill, 1)

            def bound(b):
                for j in range(NORMS):
                    pe.wait_ge(squares_ready, QK * b + j + 1)
                    if j >= 2:
                        pe.wait_ge(norm_free, NORMS * b + j - 1)
                    mm(bank[ACC + j % 2], blocks[:, :], squares[:, j // 2, (j % 2) * HALF:(j % 2 + 1) * HALF],
                       True, True).then_inc(norm_fill, 1)

            def attention(b, first):
                if first:
                    pe.wait_ge(flag_ready, 1)
                general = pe.value_load(flag[0:1, 0:1], min_val=0, max_val=1)
                pe.wait_ge(pre_free, PRE * (b + 1))
                pe.wait_ge(norm_free, NORMS * (b + 1))
                if not first:
                    pe.wait_ge(post_free, POST * b)
                pe.wait_ge(stacks_loaded, 16 * LOADS * (b + 1))
                kflat = kstack[0:ROWS, :, :].rearrange("r h n -> r (h n)")
                qflat = qstack[0:ROWS, :, :].rearrange("r h n -> r (h n)")
                with pe.If(general == 1):
                    with pe.Fori(0, HEADS) as h:
                        for t in range(TILES):
                            pe.wait_ge(gen_free, GEN_FREE * b + TILES * h + t + 1)
                            for hf in range(HALVES):
                                ins = mm(scores[t % 2][:, hf, :], kflat[:, bass.ds(TOKENS * h + P * t, P)],
                                         qflat[:, bass.ds(TOKENS * h + HALF * hf, HALF)], True, True)
                            ins.then_inc(gen_fill, 1)
                    pe.wait_ge(gen_free, GEN_FREE * (b + 1))
                    flip(bank[TR][:, 0:P], rowmax[:, :]).then_inc(gen_fill, 1)
                with pe.Else():
                    pe.sem_inc(gen_fill, GEN_FILL)
                pe.wait_ge(shift_loaded, 16 * SHIFT_ROWS * (b + 1))

                def score(u):
                    k, h = u // GROUP, u % GROUP
                    g, t = k // TILES, k % TILES
                    head = g * GROUP + h
                    if u >= 2:
                        pe.wait_ge(probs_ready, UNITS * b + u - 1)
                    for hf in range(HALVES):
                        ins = mm(scores[u % 2][:, hf, :], qstack[:, head, t * P:(t + 1) * P],
                                 kstack[:, head, hf * HALF:(hf + 1) * HALF], True, True)
                    ins.then_inc(scores_ready, 1)

                def products(k, hf):
                    g, t = k // TILES, k % TILES
                    if hf == 0:
                        pe.wait_ge(probs_ready, UNITS * b + GROUP * (k + 1))
                    if t == 0 and (g >= 1 or not first):
                        pe.wait_ge(acc_copied, 2 * GROUPS * b + 2 * (g - 1) + hf + 1)
                    for h in range(GROUP):
                        ins = mm(bank[ACC + hf][VW * h:VW * (h + 1), :], v[:, t, g * GROUP + h, :],
                                 probs[:, k % 2, h, hf * HALF:(hf + 1) * HALF], t == 0, t == TILES - 1)
                    ins.then_inc(pv_done, 1)

                for k in range(STEPS):
                    score(GROUP * k)
                    score(GROUP * k + 1)
                    if k:
                        products(k - 1, 0)
                    score(GROUP * k + 2)
                    score(GROUP * k + 3)
                    if k:
                        products(k - 1, 1)
                    if k % TILES == 2 and k > TILES:
                        turn_group(b, k // TILES - 1, first)
                products(STEPS - 1, 0)
                products(STEPS - 1, 1)

            def turn_group(b, g, first):
                for hf in range(HALVES):
                    pe.wait_ge(acc_copied, 2 * GROUPS * b + 2 * g + hf + 1)
                    if g >= 1 or not first:
                        pe.wait_ge(tr_free, 2 * GROUPS * b + 2 * (g - 1) + hf + 1)
                    for i in range(TPH):
                        c = hf * HALF + i * P
                        ins = flip(bank[TR + hf][:, i * P:(i + 1) * P], accT[:, c:c + P])
                    ins.then_inc(tr_fill, 1)

            def post(b, first, last):
                def slot(f):
                    if f >= 4:
                        pe.wait_ge(post_free, POST * b + f - 3)

                turn_group(b, GROUPS - 1, first)
                if last:
                    pe.wait_ge(probs_ready, UNITS * (b + 1))
                else:
                    pe.wait_ge(pre_free, PRE * (b + 2))
                pe.wait_ge(tr_free, 2 * GROUPS * (b + 1))
                for f in range(4):
                    hf, c = f // 2, f % 2
                    for i in range(TPH):
                        ins = flip(bank[f][:, i * P:(i + 1) * P], attn[:, hf * TPH + i, c * P:(c + 1) * P])
                    ins.then_inc(post_fill, 1)
                for j in range(4):
                    f = O0 + j
                    pe.wait_ge(post_free, POST * b + max(2 * (j // 2) + 2, f - 3))
                    for i in range(2):
                        t = 2 * j + i
                        for k in range(CHUNKS):
                            ins = mm(bank[f % 4][:, i * DIM:(i + 1) * DIM], attnT[:, k, t * P:(t + 1) * P],
                                     WoT[:, k, :], k == 0, k == CHUNKS - 1)
                    ins.then_inc(post_fill, 1)
                if not last:
                    bound(b + 1)
                for j in range(4):
                    hf, c, f = j // 2, j % 2, X0 + j
                    slot(f)
                    pe.wait_ge(x1_ready, 4 * b + 2 * hf + 2)
                    for i in range(TPH):
                        ins = flip(bank[f % 4][:, i * P:(i + 1) * P], x_res[:, hf * TPH + i, c * P:(c + 1) * P])
                    ins.then_inc(post_fill, 1)
                for g in range(2 * HCHUNKS):
                    hf, hc = g // HCHUNKS, g % HCHUNKS
                    for n, w in enumerate((gateT, upT)):
                        f = G0 + 2 * g + n
                        slot(f)
                        if g == 0:
                            pe.wait_ge(post_free, POST * b + X0 + 2)
                        if g == 2 and n == 0 and not last:
                            pe.wait_ge(flag_ready, b + 2)
                        for k in range(CHUNKS):
                            ins = mm(bank[f % 4], w[:, k, hc * P:(hc + 1) * P], xT[:, k, hf * HALF:(hf + 1) * HALF],
                                     k == 0, k == CHUNKS - 1)
                        ins.then_inc(post_fill, 1)
                for j in range(4):
                    f, hf = D0 + j, j // 2
                    slot(f)
                    pe.wait_ge(post_free, POST * b + G0 + 2 * HCHUNKS * (hf + 1))
                    for i in range(2):
                        t = (2 * j + i) % TPH
                        for hc in range(HCHUNKS):
                            ins = mm(bank[f % 4][:, i * DIM:(i + 1) * DIM], hT[hf][:, hc, t * P:(t + 1) * P],
                                     downT[:, hc, :], hc == 0, hc == HCHUNKS - 1)
                    ins.then_inc(post_fill, 1)

            pre(0, True)
            bound(0)

            def batch(b, first, last):
                attention(b, first)
                if not last:
                    pre(b + 1, False)
                post(b, first, last)

            batch(0, True, False)
            with pe.Fori(1, BATCHES - 1) as b:
                batch(b, False, False)
            batch(BATCHES - 1, False, True)


_INS = ["L0_attn_x", "L0_attn_Wq", "L0_attn_bq", "L0_attn_Wk", "L0_attn_bk", "L0_attn_Wv", "L0_attn_bv",
        "L0_attn_Wo", "L0_attn_bo", "L0_ffn_w_gate", "L0_ffn_w_up", "L0_ffn_w_down"]


def kernel(**inputs):
    import numpy as _np
    import concourse.bacc as _bacc
    from concourse import mybir as _mybir
    from concourse.bass_utils import run_bass_kernel_spmd as _run

    nc = _bacc.Bacc("TRN2", target_bir_lowering=False, num_devices=1)
    arrays, args = {}, []
    for name in _INS:
        a = _np.ascontiguousarray(inputs[name])
        arrays[f"in_{name}"] = a
        args.append(nc.dram_tensor(f"in_{name}", a.shape, _mybir.dt.from_np(a.dtype), kind="ExternalInput").ap())
    args.append(nc.dram_tensor("out_0", (BATCHES, TOKENS, DIM), _mybir.dt.float32, kind="ExternalOutput").ap())
    build(nc, *args)
    r = _run(nc, [arrays], core_ids=[0])
    return r.results[0]["out_0"]
```

```python
from contextlib import ExitStack

import concourse.bass as bass
from concourse import mybir

F32 = mybir.dt.float32
F16 = mybir.dt.float16
BF16 = mybir.dt.bfloat16
I32 = mybir.dt.int32
ALU = mybir.AluOpType
ACT = mybir.ActivationFunctionType
AX_X = mybir.AxisListType.X
RMAX = bass.bass_isa.ReduceOp.max

P = 128
BATCHES = 16
TOKENS = 1024
DIM = 256
HIDDEN = 768
HEADS = 16
HEAD_DIM = DIM // HEADS
TILES = TOKENS // P
CHUNKS = DIM // P
HCHUNKS = HIDDEN // P
HALF = 512
HALVES = TOKENS // HALF
TPH = TILES // HALVES
GROUP = 4
GROUPS = HEADS // GROUP
CHEADS = P // HEAD_DIM
VW = 2 * HEAD_DIM
EPS = 1e-5
SCORE_SCALE = 1.0 / 16.0
SCORE_BOUND = 40.0
NORM_MARGIN = 1.02
NORM_LIMIT = (SCORE_BOUND / SCORE_SCALE) ** 2
W_SCALE = 1.0 / 127.0
W_EXACT = 256.0
H_SCALE = 2.0 ** 14 / (2.0 * 256.0 * 256.0)

Q_PARTS = (0, 0, 0, 1, 1, 2)
K_PARTS = (0, 1, 2, 0, 1, 0)
ROWS = len(Q_PARTS) * HEAD_DIM
SHIFT_ROWS = 3

UNITS = HEADS * TILES
STEPS = GROUPS * TILES
PREPARE = 4

QK = 8
NEXT_ITEMS = ([(-1, "xT", j) for j in range(4)] + [(j, "qk", j) for j in range(QK)]
              + [(15 + j // 2 if j < 4 else 16 + j, "norm", j) for j in range(QK)] + [(STEPS, "v", j) for j in range(4)])
OUT_ITEMS = [((11, 20, 27)[g] + j, "out", 4 * g + j) for g in range(GROUPS - 1) for j in range(4)]
FIRST = [item[1:] for item in NEXT_ITEMS]
ITEMS = sorted(NEXT_ITEMS + OUT_ITEMS, key=lambda item: item[0])
LAST_ITEMS = OUT_ITEMS
ON_SCALAR = ("xT", "v")
PER_LIST = 8
DECIDE = 24
RELOAD = 28


def base(b):
    return len(FIRST) + len(ITEMS) * b


def freed(b):
    return len(FIRST) - PER_LIST + (len(ITEMS) - PER_LIST) * b


def rank(items, at):
    return sum((item[-2] in ON_SCALAR) == (items[at][-2] in ON_SCALAR) for item in items[:at + 1])


def place(items, kind, n):
    return [item[-2:] for item in items].index((kind, n))


def before(items, step):
    return sum(item[0] < step and item[1] not in ON_SCALAR for item in items)


POST_FILLS = ([("out", j) for j in range(4)] + [("x1T", 0), ("x1T", 1)]
              + [(w, g) for g in range(2) for w in ("gate", "up")] + [("x1T", 2), ("x1T", 3)]
              + [(w, g) for g in range(2, 2 * HCHUNKS) for w in ("gate", "up")] + [("down", j) for j in range(4)])
POST = len(POST_FILLS)
AT = {what: f for f, what in enumerate(POST_FILLS)}

LOADS = 2 * len(Q_PARTS)
GEN_FILL = GROUP * TILES * HALVES + 1
GEN_FREE = GROUP * TILES * HALVES + 3


def build(nc, x, Wq, bq, Wk, bk, Wv, bv, Wo, bo, w_gate, w_up, w_down, out):
    ctx = ExitStack()
    with ctx:
        def sb(name, shape, dt=F32):
            return ctx.enter_context(nc.sbuf_tensor(name, shape, dt))

        def sem(name):
            return ctx.enter_context(nc.semaphore(name))

        qstack = sb("qstack", [ROWS + SHIFT_ROWS, 2, GROUP, TOKENS], BF16)
        kstack = sb("kstack", [ROWS + SHIFT_ROWS, 2, GROUP, TOKENS], BF16)
        probs = sb("probs", [P, 2, GROUP, TOKENS])
        v = sb("v", [P, TILES, HEADS, VW])
        x_pre = sb("x_pre", [P, TILES, DIM])
        x_res = sb("x_res", [P, TILES, DIM])
        xT = sb("xT", [P, CHUNKS, TOKENS])
        parts = sb("parts", [P, 2, 3, TOKENS], BF16)
        rest = sb("rest", [P, 2, HALF])
        squares = sb("squares", [P, 4, TOKENS], BF16)
        pv = sb("pv", [P, HALVES, HALF])
        inv = sb("inv", [P, HALVES, HALF])
        outT = sb("outT", [P, GROUPS, TOKENS])
        h32 = sb("h32", [P, 2, HALF])
        WqT = sb("WqT", [P, CHUNKS, DIM])
        WkT = sb("WkT", [P, CHUNKS, DIM])
        WvT = sb("WvT", [P, CHUNKS, DIM])
        WoT = sb("WoT", [P, GROUPS, DIM])
        gateT = sb("gateT", [P, 3, CHUNKS * HIDDEN], BF16)
        upT = sb("upT", [P, 3, CHUNKS * HIDDEN], BF16)
        downT = sb("downT", [P, 3, HCHUNKS * DIM], BF16)
        bqk = sb("bqk", [P, 4])
        bv_col = sb("bv_col", [P, CHUNKS])
        bo_all = sb("bo_all", [P, DIM])
        ident = sb("ident", [P, P])
        blocks = sb("blocks", [P, P], BF16)
        norms = sb("norms", [P, QK])
        norm2 = sb("norm2", [P, 2])
        norm2_safe = sb("norm2_safe", [P, 2])
        norm2_all = sb("norm2_all", [P, 2])
        flag = sb("flag", [P, 1], I32)
        halfmax = sb("halfmax", [P, GROUP * TILES * HALVES])
        rowmax = sb("rowmax", [P, P])
        shift = sb("shift", [P, 2, P])
        shift_parts = sb("shift_parts", [GROUP * TILES, SHIFT_ROWS, P], BF16)
        stats = sb("stats", [P, TILES, 6])
        meanvar = sb("meanvar", [P, TILES, 2])
        vareps = sb("vareps", [P, TILES])
        rstd = sb("rstd", [P, TILES])
        minus_half = sb("minus_half", [P, TILES])
        eps = sb("eps", [P, TILES])
        margin = sb("margin", [P, 2])
        wmax = sb("wmax", [P, 3])
        wmax_all = sb("wmax_all", [P, 3])
        wtmp = sb("wtmp", [P, 3])
        h_scale = sb("h_scale", [P, 1])
        down_scale = sb("down_scale", [P, 1])
        wide = sb("wide", [P, 1], I32)

        flat = probs[:, :, :, :].rearrange("p a g n -> p (a g n)")
        H = HCHUNKS * HALF
        flat16 = flat.bitcast(F16)
        hT = [[flat16[:, (2 * s + i) * H:(2 * s + i + 1) * H].rearrange("p (c n) -> p c n", c=HCHUNKS)
               for i in range(2)] for s in range(HALVES)]
        tanh_out = [flat[:, 2 * H + s * HALF:2 * H + (s + 1) * HALF] for s in range(2)]
        gated = [flat[:, 2 * H + (2 + s) * HALF:2 * H + (3 + s) * HALF] for s in range(2)]
        out16 = outT[:, :, :].rearrange("p g n -> p (g n)").bitcast(F16)
        x1T = [out16[:, i * CHUNKS * TOKENS:(i + 1) * CHUNKS * TOKENS].rearrange("p (c n) -> p c n", c=CHUNKS)
               for i in range(2)]
        w4_raw = flat[:, 0:2048].rearrange("p (w c n) -> p w c n", w=4, c=CHUNKS)
        ints = flat[:, 2048:2048 + 3 * 1536]
        gate_raw = flat[:, 2048:3584].rearrange("p (c n) -> p c n", c=HCHUNKS)
        up_raw = flat[:, 3584:5120].rearrange("p (c n) -> p c n", c=HCHUNKS)
        down_raw = flat[:, 5120:6656].rearrange("p (c n) -> p c n", c=CHUNKS)
        wo_plain = flat[:, 6656:7168]
        w_rest = [flat[:, 7168:7680], flat[:, 7680:8192]]

        psum = ctx.enter_context(nc.psum_tensor("psum", [P, 8, HALF], F32))
        bank = [psum[:, i, :] for i in range(8)]
        scores = [psum[:, 2 * s:2 * s + 2, :] for s in range(2)]
        ACC, RING = 4, 6

        parts_dram = nc.dram_tensor("parts_dram", (BATCHES, 4, 3, P, TOKENS), BF16, kind="Internal").ap()

        bv_spread, wo_bv_made, bo_ready = sem("bv_spread"), sem("wo_bv_made"), sem("bo_ready")
        weights_loaded, ints_loaded, biases_loaded = sem("weights_loaded"), sem("ints_loaded"), sem("biases_loaded")
        wmax_ready, wmax_reduced, wide_ready = sem("wmax_ready"), sem("wmax_reduced"), sem("wide_ready")
        wo_zeroed, wo_placed = sem("wo_zeroed"), sem("wo_placed")
        consts_ready = sem("consts_ready")
        pool_step, dve_step = sem("pool_step"), sem("dve_step")
        setup_fill, setup_free = sem("setup_fill"), sem("setup_free")
        x_pre_loaded, x_res_loaded, x_res_biased = sem("x_pre_loaded"), sem("x_res_loaded"), sem("x_res_biased")
        work_fill, work_free, act_free = sem("work_fill"), sem("work_free"), sem("act_free")
        hi_ready, mid_ready, lo_ready, squares_ready = sem("hi_ready"), sem("mid_ready"), sem("lo_ready"), sem("squares_ready")
        parts_stored = [sem("parts_stored0"), sem("parts_stored1")]
        stack_loaded = [sem("stack_loaded0"), sem("stack_loaded1")]
        norm2_ready, norm2_reduced, flag_ready = sem("norm2_ready"), sem("norm2_reduced"), sem("flag_ready")
        gen_fill, gen_free = sem("gen_fill"), sem("gen_free")
        shift_ready, shift_loaded = sem("shift_ready"), sem("shift_loaded")
        scores_ready, probs_ready, pv_done = sem("scores_ready"), sem("probs_ready"), sem("pv_done")
        acc_free, sums_ready, inv_ready, out_ready = sem("acc_free"), sem("sums_ready"), sem("inv_ready"), sem("out_ready")
        post_fill, post_free = sem("post_fill"), sem("post_free")
        x1_hi_ready, tanh_ready, h_hi_ready, h_lo_ready = sem("x1_hi_ready"), sem("tanh_ready"), sem("h_hi_ready"), sem("h_lo_ready")
        stats_ready, rstd_ready, x1_ready, y_ready = sem("stats_ready"), sem("rstd_ready"), sem("x1_ready"), sem("y_ready")
        out_stored = sem("out_stored")

        x_v = x.rearrange("b (p t) d -> b p t d", t=TILES)
        out_v = out.rearrange("b (p t) d -> b p t d", t=TILES)

        block = ctx.enter_context(nc.Block())

        @block.sync
        def _(sp):
            for n, w in enumerate((Wq, Wk, Wv, Wo)):
                sp.dma_start(w4_raw[:, n, :, :], w.rearrange("(c p) k -> p c k", p=P)).then_inc(weights_loaded, 16)
            for dst, w in ((gate_raw, w_gate), (up_raw, w_up), (down_raw, w_down)):
                sp.dma_start(dst.bitcast(I32), w.rearrange("(c p) k -> p c k", p=P)).then_inc(ints_loaded, 16)
            sp.dma_start(x_pre[:, :, :], x_v[0]).then_inc(x_pre_loaded, 16)
            with nc.allow_non_contiguous_dma(reason="three bias vectors, once"):
                sp.dma_start(bqk[:, 0:2], bq.rearrange("(c p) -> p c", p=P)).then_inc(biases_loaded, 16)
                sp.dma_start(bv_col[:, :], bv.rearrange("(c p) -> p c", p=P)).then_inc(biases_loaded, 16)
                sp.dma_start(bqk[:, 2:4], bk.rearrange("(c p) -> p c", p=P)).then_inc(biases_loaded, 16)
            sp.dma_start(bo_all[:, :], bo.partition_broadcast(P)).then_inc(biases_loaded, 16)
            sp.wait_ge(setup_free, 4)
            sp.wait_ge(wo_zeroed, 1)
            for head in range(HEADS):
                c, r = head // CHEADS, (head % CHEADS) * HEAD_DIM
                g, to = head // GROUP, (head % GROUP) * VW
                sp.dma_start(WoT[to:to + HEAD_DIM, g, :], wo_plain[r:r + HEAD_DIM, c * DIM:(c + 1) * DIM]
                             ).then_inc(wo_placed, 16)

            def store_parts(b, idx):
                sp.wait_ge(lo_ready, QK * b + 2 * idx + 2)
                sp.wait_ge(squares_ready, QK * b + 2 * idx + 2)
                sp.dma_start(parts_dram[b, idx].rearrange("j p n -> p j n"), parts[:, idx % 2, :, :]
                             ).then_inc(parts_stored[idx % 2], 16)

            def load_stack(b, g):
                slot, c, at = g % 2, g // 2, (g % 2) * GROUP
                for t, (stack, which) in enumerate(((qstack, Q_PARTS), (kstack, K_PARTS))):
                    src = parts_dram[b, 2 * t + c]
                    for r, part in enumerate(which):
                        sp.dma_start(stack[r * HEAD_DIM:(r + 1) * HEAD_DIM, slot, :, :],
                                     src[part].rearrange("(h d) n -> d h n", d=HEAD_DIM)[:, at:at + GROUP, :]
                                     ).then_inc(stack_loaded[slot], 16)

            def load_shift(b, g):
                sp.wait_ge(shift_ready, GROUPS * b + g + 1)
                for r in range(SHIFT_ROWS):
                    sp.dma_start(kstack[ROWS + r:ROWS + r + 1, g % 2, :, :].rearrange("o h (t n) -> o (h t) n", t=TILES),
                                 shift_parts[:, r, :]).then_inc(shift_loaded, 16)

            for idx in range(4):
                store_parts(0, idx)
            for s in range(2):
                sp.wait_ge(parts_stored[s], 32)
            load_stack(0, 0)
            load_shift(0, 0)
            load_stack(0, 1)

            def store_result(b):
                for s in range(2):
                    sp.wait_ge(y_ready, 4 * b + 2 * (s + 1))
                    sp.dma_start(out_v[b][:, TPH * s:TPH * (s + 1), :], x_res[:, TPH * s:TPH * (s + 1), :]
                                 ).then_inc(out_stored, 16)

            def batch(b, first, last):
                if not last:
                    if first:
                        sp.wait_ge(work_fill, place(FIRST, "xT", 3) + 1)
                    else:
                        sp.wait_ge(work_fill, base(b - 1) + place(ITEMS, "xT", 3) + 1)
                    sp.dma_start(x_pre[:, :, :], x_v[b + 1]).then_inc(x_pre_loaded, 16)
                if not first:
                    store_result(b - 1)
                    sp.wait_ge(out_stored, 32 * b)
                sp.dma_start(x_res[:, :, :], x_v[b]).then_inc(x_res_loaded, 16)
                if not last:
                    store_parts(b + 1, 0)
                    store_parts(b + 1, 1)
                load_shift(b, 1)
                if not last:
                    store_parts(b + 1, 2)
                sp.wait_ge(scores_ready, UNITS * b + GROUP * TILES)
                load_stack(b, 2)
                if not last:
                    store_parts(b + 1, 3)
                load_shift(b, 2)
                sp.wait_ge(scores_ready, UNITS * b + 2 * GROUP * TILES)
                load_stack(b, 3)
                load_shift(b, 3)
                if not last:
                    sp.wait_ge(scores_ready, UNITS * b + 3 * GROUP * TILES)
                    for s in range(2):
                        sp.wait_ge(parts_stored[s], 32 * (b + 2))
                    load_stack(b + 1, 0)
                    load_shift(b + 1, 0)
                    sp.wait_ge(scores_ready, UNITS * (b + 1))
                    load_stack(b + 1, 1)

            batch(0, True, False)
            with sp.Fori(1, BATCHES - 1) as b:
                batch(b, False, False)
            batch(BATCHES - 1, False, True)
            store_result(BATCHES - 1)
            sp.wait_ge(out_stored, 32 * BATCHES)

        @block.gpsimd
        def _(pool):
            step = 0

            def then(ins):
                nonlocal step
                step += 1
                ins.then_inc(pool_step, 1)
                pool.wait_ge(pool_step, step)

            then(nc.gpsimd.memset(ident[:, :], 0.0))
            nc.gpsimd.affine_select(out=ident[:, :], in_=ident[:, :], compare_op=ALU.not_equal, fill=1.0, base=0,
                                    pattern=[[-1, P]], channel_multiplier=1).then_inc(consts_ready, 1)
            then(nc.gpsimd.memset(blocks[:, :], 1.0))
            blk = blocks[:, :].rearrange("p (h d) -> p h d", d=HEAD_DIM)
            then(nc.gpsimd.affine_select(out=blk, in_=blk, compare_op=ALU.is_ge, fill=0.0, base=0,
                                         pattern=[[-HEAD_DIM, CHEADS], [0, HEAD_DIM]], channel_multiplier=1))
            nc.gpsimd.affine_select(out=blk, in_=blk, compare_op=ALU.is_ge, fill=0.0, base=HEAD_DIM - 1,
                                    pattern=[[HEAD_DIM, CHEADS], [0, HEAD_DIM]], channel_multiplier=-1
                                    ).then_inc(consts_ready, 1)
            nc.gpsimd.memset(v[:, :, :, HEAD_DIM:], 1.0).then_inc(consts_ready, 1)
            nc.gpsimd.memset(WoT[:, :, :], 0.0).then_inc(wo_zeroed, 1)
            then(nc.gpsimd.memset(minus_half[:, :], -0.5))
            then(nc.gpsimd.memset(eps[:, :], EPS))
            then(nc.gpsimd.memset(margin[:, :], NORM_MARGIN))
            pool.wait_ge(wmax_ready, 1)
            nc.gpsimd.partition_all_reduce(wmax_all[:, :], wmax[:, :], P, RMAX).then_inc(wmax_reduced, 1)
            setup_steps = step

            def split(b):
                for j in range(QK):
                    s, idx, hf = j % 2, j // 2, j % 2
                    cols = slice(hf * HALF, (hf + 1) * HALF)
                    pool.wait_ge(mid_ready, QK * b + j + 1)
                    nc.gpsimd.tensor_tensor(parts[:, idx % 2, 2, cols], rest[:, s, :], parts[:, idx % 2, 1, cols],
                                            ALU.subtract).then_inc(lo_ready, 1)
                    nc.gpsimd.tensor_tensor(squares[:, idx, cols], parts[:, idx % 2, 0, cols],
                                            parts[:, idx % 2, 0, cols], ALU.mult).then_inc(squares_ready, 1)
                pool.wait_ge(norm2_ready, b + 1)
                nc.gpsimd.tensor_tensor(norm2_safe[:, :], norm2[:, :], margin[:, :], ALU.mult)
                pool.drain()
                nc.gpsimd.partition_all_reduce(norm2_all[:, :], norm2_safe[:, :], P, RMAX).then_inc(norm2_reduced, 1)

            def make_rstd(b, j, which):
                tiles = slice(2 * j, 2 * j + 2)
                n = TILES * b + 4 * which + j
                pool.wait_ge(stats_ready, n + 1)
                nc.gpsimd.tensor_tensor(vareps[:, tiles], meanvar[:, tiles, 1], eps[:, tiles], ALU.add
                                        ).then_inc(pool_step, 1)
                pool.wait_ge(pool_step, n + 1 + setup_steps)
                nc.gpsimd.tensor_tensor(rstd[:, tiles], vareps[:, tiles], minus_half[:, tiles], ALU.pow
                                        ).then_inc(rstd_ready, 1)

            def batch(b, last):
                pool.wait_ge(x_res_loaded, 16 * (b + 1))
                nc.gpsimd.tensor_tensor(x_res[:, :, :], x_res[:, :, :],
                                        bo_all[:, :].unsqueeze(1).to_broadcast([P, TILES, DIM]), ALU.add
                                        ).then_inc(x_res_biased, 1)
                if not last:
                    split(b + 1)
                for j in range(4):
                    make_rstd(b, j, 0)
                for g in range(2 * HCHUNKS):
                    hf, hc = g // HCHUNKS, g % HCHUNKS
                    pool.wait_ge(h_hi_ready, 2 * HCHUNKS * b + g + 1)
                    nc.gpsimd.tensor_tensor(hT[hf][1][:, hc, :], h32[:, g % 2, :], hT[hf][0][:, hc, :], ALU.subtract
                                            ).then_inc(h_lo_ready, 1)
                for j in range(4):
                    make_rstd(b, j, 1)

            split(0)
            pool.wait_ge(bo_ready, 1)
            batch(0, False)
            with pool.Fori(1, BATCHES - 1) as b:
                batch(b, False)
            batch(BATCHES - 1, True)

        @block.scalar
        def _(act):
            act.wait_ge(biases_loaded, 64)

            def hi(b, j, start, at, first):
                idx, hf = j // 2, j % 2
                act.wait_ge(work_fill, start + at + 1)
                if hf == 0 and not (first and idx < 2):
                    act.wait_ge(parts_stored[idx % 2], 32 * b + 16 * (idx // 2))
                nc.scalar.activation(parts[:, idx % 2, 0, hf * HALF:(hf + 1) * HALF], bank[RING + at % 2],
                                     ACT.Identity, bias=bqk[:, idx:idx + 1]).then_inc(hi_ready, 1)

            def mid(j, count):
                idx, hf = j // 2, j % 2
                act.wait_ge(work_free, count)
                nc.scalar.activation(parts[:, idx % 2, 1, hf * HALF:(hf + 1) * HALF], rest[:, j % 2, :],
                                     ACT.Copy).then_inc(mid_ready, 1)

            def copy_v(j, start, at):
                act.wait_ge(work_fill, start + at + 1)
                nc.scalar.activation(v[:, 2 * j:2 * j + 2, :, 0:HEAD_DIM],
                                     bank[RING + at % 2].rearrange("p (t h d) -> p t h d", t=2, d=HEAD_DIM), ACT.Copy
                                     ).then_inc(act_free, 1)

            def copy_xT(j, start, at):
                hf, c = j // 2, j % 2
                act.wait_ge(work_fill, start + at + 1)
                nc.scalar.activation(xT[:, c, hf * HALF:(hf + 1) * HALF], bank[RING + at % 2], ACT.Copy
                                     ).then_inc(act_free, 1)

            def attention(b, first, last):
                if not last:
                    for j in range(4):
                        copy_xT(j, base(b), place(ITEMS, "xT", j))
                if not first:
                    act.wait_ge(post_free, POST * b)
                for u in range(UNITS):
                    k, h = u // GROUP, u % GROUP
                    act.wait_ge(scores_ready, UNITS * b + u + 1)
                    if h == 0 and k >= 2:
                        act.wait_ge(pv_done, 2 * STEPS * b + 2 * (k - 1))
                    nc.scalar.activation(probs[:, k % 2, h, :], scores[u % 2].rearrange("p a n -> p (a n)"), ACT.Exp,
                                         scale=SCORE_SCALE).then_inc(probs_ready, 1)
                    if last:
                        continue
                    for n, (s, kind, j) in enumerate(ITEMS):
                        if kind == "qk" and s == k - 1:
                            if h == 0:
                                hi(b + 1, j, base(b), n, False)
                            if h == 2:
                                mid(j, freed(b) + rank(ITEMS, n))
                if not last:
                    act.wait_ge(pv_done, 2 * STEPS * (b + 1))
                    for j in range(4):
                        copy_v(j, base(b), place(ITEMS, "v", j))

            def post(b):
                def x1_hi(n):
                    f, hf, c = AT["x1T", n], n // 2, n % 2
                    act.wait_ge(post_fill, POST * b + f + 1)
                    nc.scalar.activation(x1T[0][:, c, hf * HALF:(hf + 1) * HALF], bank[f % 4], ACT.Copy
                                         ).then_inc(x1_hi_ready, 1)

                def tanh(g):
                    f = AT["gate", g]
                    act.wait_ge(post_fill, POST * b + f + 1)
                    if g >= 2:
                        act.wait_ge(post_free, POST * b + AT["gate", g - 2] + 1)
                    nc.scalar.activation(tanh_out[g % 2], bank[f % 4], ACT.Tanh, scale=0.5 * W_SCALE
                                         ).then_inc(tanh_ready, 1)

                def h_hi(g):
                    act.wait_ge(post_free, POST * b + AT["up", g] + 1)
                    nc.scalar.activation(hT[g // HCHUNKS][0][:, g % HCHUNKS, :], h32[:, g % 2, :], ACT.Copy
                                         ).then_inc(h_hi_ready, 1)

                for n in range(2):
                    x1_hi(n)
                for g in range(2 * HCHUNKS):
                    tanh(g)
                    if g >= 1:
                        h_hi(g - 1)
                    if g == 1:
                        for n in range(2, 4):
                            x1_hi(n)
                h_hi(2 * HCHUNKS - 1)

            for j in range(4):
                copy_xT(j, 0, place(FIRST, "xT", j))
            for j in range(QK):
                hi(0, j, 0, place(FIRST, "qk", j), True)
                mid(j, rank(FIRST, place(FIRST, "qk", j)))
            for j in range(4):
                copy_v(j, 0, place(FIRST, "v", j))

            def batch(b, first, last):
                attention(b, first, last)
                post(b)

            batch(0, True, False)
            with act.Fori(1, BATCHES - 1) as b:
                batch(b, False, False)
            batch(BATCHES - 1, False, True)

        @block.vector
        def _(dve):
            steps = 0

            def then(ins):
                nonlocal steps
                steps += 1
                ins.then_inc(dve_step, 1)
                dve.wait_ge(dve_step, steps)

            nc.vector.memset(qstack[ROWS:ROWS + SHIFT_ROWS, :, :, :], 1.0).then_inc(consts_ready, 1)
            then(nc.vector.memset(rowmax[:, :], 0.0))
            for f, t in enumerate((wo_plain, WqT, WkT, WvT)):
                dve.wait_ge(setup_fill, f + 1)
                o = t if f == 0 else t[:, :, :].rearrange("p c n -> p (c n)")
                nc.vector.tensor_copy(o, bank[f % 4]).then_inc(setup_free, 1)
            dve.wait_ge(ints_loaded, 48)
            then(nc.vector.tensor_copy(ints, ints.bitcast(I32)))
            nc.vector.tensor_reduce(wmax[:, :], ints.rearrange("p (w n) -> p w n", w=3), AX_X, ALU.max,
                                    apply_absolute_value=True).then_inc(wmax_ready, 1)
            f = 4
            for t in (gateT, upT, downT):
                for i in range(3):
                    cols = slice(i * HALF, (i + 1) * HALF)
                    dve.wait_ge(setup_fill, f + 1)
                    then(nc.vector.tensor_copy(t[:, 0, cols], bank[f % 4]))
                    ins = nc.vector.tensor_tensor(w_rest[0], bank[f % 4], t[:, 0, cols], ALU.subtract)
                    ins.then_inc(setup_free, 1)
                    dve.wait_ge(setup_free, f + 1)
                    then(nc.vector.tensor_copy(t[:, 1, cols], w_rest[0]))
                    then(nc.vector.tensor_tensor(t[:, 2, cols], w_rest[0], t[:, 1, cols], ALU.subtract))
                    f += 1
            dve.wait_ge(wmax_reduced, 1)
            then(nc.vector.tensor_scalar(wmax[:, :], wmax_all[:, :], 1.0, None, ALU.max))
            then(nc.vector.tensor_scalar(wtmp[:, 0:1], wmax[:, 0:1], wmax[:, 1:2], None, ALU.mult))
            then(nc.vector.reciprocal(wtmp[:, 1:2], wtmp[:, 0:1]))
            then(nc.vector.tensor_scalar(h_scale[:, :], wtmp[:, 1:2], H_SCALE, None, ALU.mult))
            then(nc.vector.tensor_scalar(down_scale[:, :], wtmp[:, 0:1], 0.5 * W_SCALE ** 3 / H_SCALE, None, ALU.mult))
            then(nc.vector.tensor_reduce(wtmp[:, 2:3], wmax[:, :], AX_X, ALU.max))
            nc.vector.tensor_scalar(wide[:, :], wtmp[:, 2:3], W_EXACT, None, ALU.is_gt).then_inc(wide_ready, 1)
            dve.wait_ge(biases_loaded, 64)
            dve.wait_ge(consts_ready, 4)
            for c in range(CHUNKS):
                ins = nc.vector.tensor_scalar(rest[:, 0, c * P:(c + 1) * P], ident[:, :], 0.0, bv_col[:, c:c + 1],
                                              ALU.mult, ALU.add)
            ins.then_inc(bv_spread, 1)
            dve.wait_ge(wo_bv_made, 1)
            nc.vector.tensor_tensor(bo_all[:, :], bank[ACC][:, 0:DIM], bo_all[:, :], ALU.add).then_inc(bo_ready, 1)

            def take_work(b, kind, j, n, bank_of, first):
                o = bank[RING + bank_of]
                if kind == "qk":
                    idx, hf = j // 2, j % 2
                    dve.wait_ge(hi_ready, QK * b + j + 1)
                    if j >= 2 or not first:
                        dve.wait_ge(lo_ready, QK * b + j - 1)
                    nc.vector.scalar_tensor_tensor(out=rest[:, j % 2, :], in0=o, scalar=bqk[:, idx:idx + 1],
                                                   in1=parts[:, idx % 2, 0, hf * HALF:(hf + 1) * HALF],
                                                   op0=ALU.add, op1=ALU.subtract).then_inc(work_free, 1)
                elif kind == "norm":
                    dve.wait_ge(work_fill, n + 1)
                    nc.vector.tensor_reduce(norms[:, j:j + 1], o, AX_X, ALU.max).then_inc(work_free, 1)
                    if j == QK - 1:
                        dve.drain()
                        nc.vector.tensor_reduce(norm2[:, :], norms[:, :].rearrange("p (t j) -> p t j", t=2), AX_X,
                                                ALU.max).then_inc(norm2_ready, 1)
                elif kind == "out":
                    if j == 0:
                        dve.wait_ge(x_res_biased, b + 1)
                    dve.wait_ge(work_fill, n + 1)
                    i = 2 * (j % 4)
                    tiles = x_res[:, i:i + 2, :].rearrange("p t d -> p (t d)")
                    nc.vector.tensor_tensor(tiles, o, tiles, ALU.add).then_inc(work_free, 1)

            def decide(b):
                dve.wait_ge(norm2_reduced, b + 1)
                nc.vector.tensor_scalar(flag[:, :], norm2_all[:, 0:1], norm2_all[:, 1:2], NORM_LIMIT, ALU.mult,
                                        ALU.is_ge).then_inc(flag_ready, 1)

            general = dve.alloc_register("dve_general")

            def prepare_shift(n, first=False):
                with dve.If_eq(general, 1):
                    dve.sem_inc(gen_free, 2)
                    with dve.Fori(0, GROUP) as h:
                        for w in range(TILES * HALVES):
                            dve.wait_ge(gen_fill, GEN_FILL * n + TILES * HALVES * h + w + 1)
                            nc.vector.tensor_reduce(halfmax[:, bass.ds(TILES * HALVES * h + w, 1)], bank[RING + w % 2],
                                                    AX_X, ALU.max).then_inc(gen_free, 1)
                    dve.drain()
                    nc.vector.tensor_reduce(rowmax[:, 0:GROUP * TILES],
                                            halfmax[:, :].rearrange("p (n f) -> p n f", f=HALVES), AX_X, ALU.max
                                            ).then_inc(gen_free, 1)
                    R = GROUP * TILES
                    dve.wait_ge(gen_fill, GEN_FILL * (n + 1))
                    nc.vector.tensor_scalar(shift[0:R, 0, :], bank[RING][0:R, 0:P], -1.0, None, ALU.mult)
                    dve.drain()
                    if not first:
                        dve.wait_ge(shift_loaded, 16 * SHIFT_ROWS * n)
                    nc.vector.tensor_copy(shift_parts[:, 0, :], shift[0:R, 0, :])
                    dve.drain()
                    nc.vector.tensor_tensor(shift[0:R, 1, :], shift[0:R, 0, :], shift_parts[:, 0, :], ALU.subtract)
                    dve.drain()
                    nc.vector.tensor_copy(shift_parts[:, 1, :], shift[0:R, 1, :])
                    dve.drain()
                    nc.vector.tensor_tensor(shift_parts[:, 2, :], shift[0:R, 1, :], shift_parts[:, 1, :],
                                            ALU.subtract).then_inc(shift_ready, 1)
                with dve.Else():
                    dve.sem_inc(gen_free, GEN_FREE)
                    if not first:
                        dve.wait_ge(shift_loaded, 16 * SHIFT_ROWS * n)
                    nc.vector.memset(shift_parts[:, :, :], 0.0).then_inc(shift_ready, 1)

            take_sums = [HEAD_DIM + i % HEAD_DIM for i in range(VW)]

            def take_group(b, g):
                def copy(hf):
                    dve.wait_ge(pv_done, 2 * STEPS * b + 2 * (TILES * (g + 1) - 1) + hf + 1)
                    nc.vector.tensor_copy(pv[:, hf, :], bank[ACC + hf]).then_inc(acc_free, 1)

                def divide(hf):
                    n = 2 * GROUPS * b + 2 * g + hf + 1
                    dve.drain()
                    nc.vector.stream_shuffle(inv[:, hf, :], pv[:, hf, :], take_sums).then_inc(sums_ready, 1)
                    dve.wait_ge(sums_ready, n)
                    nc.vector.reciprocal(inv[:, hf, :], inv[:, hf, :]).then_inc(inv_ready, 1)
                    dve.wait_ge(inv_ready, n)
                    nc.vector.tensor_tensor(outT[:, g, hf * HALF:(hf + 1) * HALF], pv[:, hf, :], inv[:, hf, :],
                                            ALU.mult).then_inc(out_ready, 1)

                copy(0)
                if g == GROUPS - 1:
                    divide(0)
                    copy(1)
                else:
                    copy(1)
                    divide(0)
                divide(1)

            def add_and_stats(b, what, j, scale):
                f = AT[what, j]
                tiles = x_res[:, 2 * j:2 * j + 2, :].rearrange("p t d -> p (t d)")
                dve.wait_ge(post_fill, POST * b + f + 1)
                nc.vector.scalar_tensor_tensor(out=tiles, in0=bank[f % 4], scalar=scale, in1=tiles, op0=ALU.mult,
                                               op1=ALU.add).then_inc(post_free, 1)
                dve.wait_ge(post_free, POST * b + f + 1)
                for i in range(2):
                    nc.vector.bn_stats(stats[:, 2 * j + i, :], x_res[:, 2 * j + i, :])
                dve.drain()
                for i in range(2):
                    ins = nc.vector.bn_aggr(meanvar[:, 2 * j + i, :], stats[:, 2 * j + i, :])
                ins.then_inc(stats_ready, 1)

            def normalise(b, j, which, done):
                dve.wait_ge(rstd_ready, TILES * b + 4 * which + j + 1)
                for i in range(2):
                    t = 2 * j + i
                    ins = nc.vector.tensor_scalar(x_res[:, t, :], x_res[:, t, :], meanvar[:, t, 0:1],
                                                  rstd[:, t:t + 1], ALU.subtract, ALU.mult)
                ins.then_inc(done, 1)

            def post(b):
                def x1_lo(n):
                    f, hf, c = AT["x1T", n], n // 2, n % 2
                    dve.wait_ge(x1_hi_ready, 4 * b + n + 1)
                    cols = slice(hf * HALF, (hf + 1) * HALF)
                    nc.vector.tensor_tensor(x1T[1][:, c, cols], bank[f % 4], x1T[0][:, c, cols], ALU.subtract
                                            ).then_inc(post_free, 1)

                def gate(g):
                    f = AT["gate", g]
                    dve.wait_ge(tanh_ready, 2 * HCHUNKS * b + g + 1)
                    nc.vector.scalar_tensor_tensor(out=gated[g % 2], in0=tanh_out[g % 2], scalar=1.0, in1=bank[f % 4],
                                                   op0=ALU.add, op1=ALU.mult).then_inc(post_free, 1)
                    dve.wait_ge(post_fill, POST * b + f + 2)
                    dve.wait_ge(post_free, POST * b + f + 1)
                    if g >= 2:
                        dve.wait_ge(h_lo_ready, 2 * HCHUNKS * b + g - 1)
                    nc.vector.scalar_tensor_tensor(out=h32[:, g % 2, :], in0=gated[g % 2], scalar=h_scale[:, 0:1],
                                                   in1=bank[(f + 1) % 4], op0=ALU.mult, op1=ALU.mult
                                                   ).then_inc(post_free, 1)

                for j in range(4):
                    add_and_stats(b, "out", j, 1.0)
                    if j >= 1:
                        normalise(b, j - 1, 0, x1_ready)
                normalise(b, 3, 0, x1_ready)
                x1_lo(0)
                x1_lo(1)
                for g in range(2 * HCHUNKS):
                    gate(g)
                    if g == 1:
                        x1_lo(2)
                        x1_lo(3)
                for j in range(4):
                    add_and_stats(b, "down", j, down_scale[:, 0:1])
                    if j >= 1:
                        normalise(b, j - 1, 1, y_ready)
                normalise(b, 3, 1, y_ready)

            def batch(b, first, last):
                items = LAST_ITEMS if last else ITEMS

                def take_items(step):
                    for n, (s, kind, j) in enumerate(items):
                        if s == step:
                            take_work(b if kind == "out" else b + 1, kind, j, base(b) + n, n % 2, False)

                take_items(-1)
                for k in range(STEPS):
                    if k == DECIDE and not last:
                        decide(b + 1)
                        dve.wait_ge(flag_ready, b + 2)
                    if k % TILES == 0 and k:
                        take_group(b, k // TILES - 1)
                    if k == RELOAD and not last:
                        dve.reg_load(general, flag[0:1, 0:1])
                    if k % TILES == PREPARE and not (last and k // TILES == GROUPS - 1):
                        prepare_shift(GROUPS * b + k // TILES + 1)
                    take_items(k)
                take_group(b, GROUPS - 1)
                post(b)

            for n, (kind, j) in enumerate(FIRST):
                take_work(0, kind, j, n, n % 2, True)
            decide(0)
            dve.wait_ge(flag_ready, 1)
            dve.reg_load(general, flag[0:1, 0:1])
            prepare_shift(0, True)
            batch(0, True, False)
            with dve.Fori(1, BATCHES - 1) as b:
                batch(b, False, False)
            batch(BATCHES - 1, False, True)

        @block.tensor
        def _(pe):
            def mm(o, lhsT, rhs, start, stop):
                return nc.tensor.matmul(o, lhsT, rhs, start=start, stop=stop)

            def flip(o, src):
                return nc.tensor.transpose(o, src, ident[:, :])

            pe.wait_ge(consts_ready, 4)
            pe.wait_ge(weights_loaded, 16 * 4)
            tiles = []
            for n in (3, 0, 1, 2):
                tiles += [w4_raw[:, n, o, k * P:(k + 1) * P] for k in range(CHUNKS) for o in range(CHUNKS)]
            for raw in (gate_raw, up_raw):
                tiles += [raw[:, hc, k * P:(k + 1) * P] for k in range(CHUNKS) for hc in range(HCHUNKS)]
            tiles += [down_raw[:, c, hc * P:(hc + 1) * P] for hc in range(HCHUNKS) for c in range(CHUNKS)]
            fills = len(tiles) // 4
            for f in range(fills):
                if f == 4:
                    pe.wait_ge(wmax_ready, 1)
                if f >= 4:
                    pe.wait_ge(setup_free, f - 3)
                for i in range(4):
                    ins = flip(bank[f % 4][:, i * P:(i + 1) * P], tiles[4 * f + i])
                ins.then_inc(setup_fill, 1)

            pe.wait_ge(bv_spread, 1)
            for c in range(CHUNKS):
                ins = mm(bank[ACC][:, 0:DIM], rest[:, 0, c * P:(c + 1) * P], wo_plain[:, c * DIM:(c + 1) * DIM],
                         c == 0, c == CHUNKS - 1)
            ins.then_inc(wo_bv_made, 1)

            general = pe.alloc_register("pe_general")
            wide_weights = pe.alloc_register("pe_wide")

            def do_work(b, items, at, half=None):
                kind, j = items[at][-2:]
                o = bank[RING + at % 2]
                data = 0 if items is FIRST else b if kind == "out" else b + 1
                by_dve, by_act = (0, 0) if items is FIRST else (freed(b), PER_LIST * b + PER_LIST)
                halves = range(2) if half is None else (half,)
                if half != 1:
                    if at >= 2 and items[at - 2][-2] in ON_SCALAR:
                        pe.wait_ge(act_free, by_act + rank(items, at - 2))
                    elif at >= 2:
                        pe.wait_ge(work_free, by_dve + rank(items, at - 2))
                    elif items is not FIRST:
                        pe.wait_ge(act_free, PER_LIST * b + PER_LIST - 1 + at)
                if kind == "xT":
                    hf, c = j // 2, j % 2
                    if j == 0 and half != 1:
                        pe.wait_ge(x_pre_loaded, 16 * (data + 1))
                    for i in [2 * m + i for m in halves for i in range(2)]:
                        ins = flip(o[:, i * P:(i + 1) * P], x_pre[:, hf * TPH + i, c * P:(c + 1) * P])
                elif kind == "qk":
                    idx, hf = j // 2, j % 2
                    w, c = (WqT, WkT)[idx // 2], idx % 2
                    if j == 0 and half != 1:
                        pe.wait_ge(act_free, by_act + 4)
                    for k in halves:
                        ins = mm(o, w[:, k, c * P:(c + 1) * P], xT[:, k, hf * HALF:(hf + 1) * HALF],
                                 k == 0, k == CHUNKS - 1)
                elif kind == "norm":
                    if half != 1:
                        pe.wait_ge(squares_ready, QK * data + j + 1)
                        ins = mm(o, blocks[:, :], squares[:, j // 2, (j % 2) * HALF:(j % 2 + 1) * HALF], True, True)
                        ins.then_inc(work_fill, 1)
                    return
                elif kind == "v":
                    for i in halves:
                        t = 2 * j + i
                        for k in range(CHUNKS):
                            ins = mm(o[:, i * DIM:(i + 1) * DIM], xT[:, k, t * P:(t + 1) * P], WvT[:, k, :],
                                     k == 0, k == CHUNKS - 1)
                elif kind == "out":
                    ins = project(b, j // 4, j % 4, o, halves)
                if half != 0:
                    ins.then_inc(work_fill, 1)

            def project(b, g, j, o, halves=range(2)):
                if j % 2 == 0 and 0 in halves:
                    pe.wait_ge(out_ready, 2 * GROUPS * b + 2 * g + j // 2 + 1)
                for i in halves:
                    t = 2 * j + i
                    ins = mm(o[:, i * DIM:(i + 1) * DIM], outT[:, g, t * P:(t + 1) * P], WoT[:, g, :], True, True)
                return ins

            def stack_here(n, slot, b, g):
                pe.wait_ge(stack_loaded[slot], 16 * LOADS * (2 * b + g // 2 + 1))

            def prepare_shift(n, b, g, work_done):
                slot = g % 2
                kflat = kstack[0:ROWS, slot, :, :].rearrange("r h n -> r (h n)")
                qflat = qstack[0:ROWS, slot, :, :].rearrange("r h n -> r (h n)")
                with pe.If_eq(general, 1):
                    with pe.Fori(0, GROUP) as h:
                        for w in range(TILES * HALVES):
                            t, hf = w // HALVES, w % HALVES
                            if w == 0:
                                stack_here(n, slot, b, g)
                                pe.wait_ge(work_free, work_done)
                            pe.wait_ge(gen_free, GEN_FREE * n + TILES * HALVES * h + w + 1)
                            mm(bank[RING + w % 2], kflat[:, bass.ds(TOKENS * h + P * t, P)],
                               qflat[:, bass.ds(TOKENS * h + HALF * hf, HALF)], True, True).then_inc(gen_fill, 1)
                    pe.wait_ge(gen_free, GEN_FREE * (n + 1))
                    flip(bank[RING][:, 0:P], rowmax[:, :]).then_inc(gen_fill, 1)
                    pe.wait_ge(shift_ready, n + 1)
                with pe.Else():
                    pe.sem_inc(gen_fill, GEN_FILL)

            def attention(b, first, last):
                items = LAST_ITEMS if last else ITEMS

                def do_items(step, half=None):
                    here = [n for n, item in enumerate(items) if item[0] == step]
                    if half is None or len(here) == 1:
                        for n in here:
                            do_work(b, items, n, half)
                    elif here:
                        do_work(b, items, here[half])

                do_items(-1)
                if not first:
                    pe.wait_ge(post_free, POST * b)

                def score(u):
                    k, h = u // GROUP, u % GROUP
                    g, t = k // TILES, k % TILES
                    if t == 0 and h == 0:
                        stack_here(GROUPS * b + g, g % 2, b, g)
                        pe.wait_ge(shift_loaded, 16 * SHIFT_ROWS * (GROUPS * b + g + 1))
                    if u >= 2:
                        pe.wait_ge(probs_ready, UNITS * b + u - 1)
                    for hf in range(HALVES):
                        ins = mm(scores[u % 2][:, hf, :], qstack[:, g % 2, h, t * P:(t + 1) * P],
                                 kstack[:, g % 2, h, hf * HALF:(hf + 1) * HALF], True, True)
                    ins.then_inc(scores_ready, 1)

                def products(k, hf):
                    g, t = k // TILES, k % TILES
                    if hf == 0:
                        pe.wait_ge(probs_ready, UNITS * b + GROUP * (k + 1))
                    if t == 0 and (g >= 1 or not first):
                        pe.wait_ge(acc_free, 2 * GROUPS * b + 2 * (g - 1) + hf + 1)
                    for h in range(GROUP):
                        ins = mm(bank[ACC + hf][VW * h:VW * (h + 1), :], v[:, t, g * GROUP + h, :],
                                 probs[:, k % 2, h, hf * HALF:(hf + 1) * HALF], t == 0, t == TILES - 1)
                    ins.then_inc(pv_done, 1)

                for k in range(STEPS):
                    if k == RELOAD and not last:
                        pe.wait_ge(flag_ready, b + 2)
                    score(GROUP * k)
                    if k == RELOAD and not last:
                        pe.reg_load(general, flag[0:1, 0:1])
                    g = k // TILES
                    if k % TILES == PREPARE and not (last and g == GROUPS - 1):
                        nb = b if g < GROUPS - 1 else b + 1
                        prepare_shift(GROUPS * b + g + 1, nb, (g + 1) % GROUPS, freed(b) + before(items, k))
                    do_items(k, 0)
                    score(GROUP * k + 1)
                    if k:
                        products(k - 1, 0)
                    score(GROUP * k + 2)
                    do_items(k, 1)
                    score(GROUP * k + 3)
                    if k:
                        products(k - 1, 1)
                products(STEPS - 1, 0)
                products(STEPS - 1, 1)

                def tail(j):
                    if not last:
                        do_work(b, items, place(items, "v", j))

                for j in range(4):
                    if j % 2 == 0:
                        tail(j)
                        tail(j + 1)
                    project(b, GROUPS - 1, j, bank[j]).then_inc(post_fill, 1)

            def post(b, last):
                def feed_forward(w_parts):
                    def ready(f):
                        return POST * b + f + 1

                    for what, n in POST_FILLS[AT["gate", 0]:]:
                        f = AT[what, n]
                        o = bank[f % 4]
                        pe.wait_ge(post_free, POST * b + f - 3)
                        if what == "x1T":
                            ins = flip_x1(f, n)
                        elif what in ("gate", "up"):
                            w = gateT if what == "gate" else upT
                            hf, hc = n // HCHUNKS, n % HCHUNKS
                            if what == "gate" and hc == 0:
                                pe.wait_ge(post_free, ready(AT["x1T", 2 * hf + 1]))
                            terms = [(k, i, part) for k in range(CHUNKS) for part in range(w_parts) for i in range(2)]
                            for m, (k, i, part) in enumerate(terms):
                                at = k * HIDDEN + hc * P
                                ins = mm(o, w[:, part, at:at + P], x1T[i][:, k, hf * HALF:(hf + 1) * HALF],
                                         m == 0, m == len(terms) - 1)
                        else:
                            hf = n // 2
                            pe.wait_ge(h_lo_ready, 2 * HCHUNKS * b + HCHUNKS * (hf + 1))
                            for s in range(2):
                                t = (2 * n + s) % TPH
                                terms = [(hc, i, part) for hc in range(HCHUNKS) for part in range(w_parts)
                                         for i in range(2)]
                                for m, (hc, i, part) in enumerate(terms):
                                    ins = mm(o[:, s * DIM:(s + 1) * DIM], hT[hf][i][:, hc, t * P:(t + 1) * P],
                                             downT[:, part, hc * DIM:(hc + 1) * DIM], m == 0, m == len(terms) - 1)
                        ins.then_inc(post_fill, 1)

                def flip_x1(f, n):
                    hf, c = n // 2, n % 2
                    pe.wait_ge(x1_ready, 4 * b + 2 * hf + 2)
                    for i in range(TPH):
                        ins = flip(bank[f % 4][:, i * P:(i + 1) * P], x_res[:, hf * TPH + i, c * P:(c + 1) * P])
                    return ins

                for n in range(2):
                    f = AT["x1T", n]
                    pe.wait_ge(post_free, POST * b + f - 3)
                    flip_x1(f, n).then_inc(post_fill, 1)
                with pe.If_eq(wide_weights, 1):
                    feed_forward(3)
                with pe.Else():
                    feed_forward(1)

            for n in range(len(FIRST)):
                do_work(0, FIRST, n)
            pe.wait_ge(wide_ready, 1)
            pe.wait_ge(flag_ready, 1)
            pe.reg_load(wide_weights, wide[0:1, 0:1])
            pe.reg_load(general, flag[0:1, 0:1])
            pe.wait_ge(act_free, PER_LIST)
            prepare_shift(0, 0, 0, freed(0))
            pe.wait_ge(setup_free, fills)
            pe.wait_ge(wo_placed, 16 * HEADS)

            def batch(b, first, last):
                attention(b, first, last)
                post(b, last)

            batch(0, True, False)
            with pe.Fori(1, BATCHES - 1) as b:
                batch(b, False, False)
            batch(BATCHES - 1, False, True)


_INS = ["L0_attn_x", "L0_attn_Wq", "L0_attn_bq", "L0_attn_Wk", "L0_attn_bk", "L0_attn_Wv", "L0_attn_bv",
        "L0_attn_Wo", "L0_attn_bo", "L0_ffn_w_gate", "L0_ffn_w_up", "L0_ffn_w_down"]


def kernel(**inputs):
    import numpy as _np
    import concourse.bacc as _bacc
    from concourse import mybir as _mybir
    from concourse.bass_utils import run_bass_kernel_spmd as _run

    nc = _bacc.Bacc("TRN2", target_bir_lowering=False, num_devices=1)
    arrays, args = {}, []
    for name in _INS:
        a = _np.ascontiguousarray(inputs[name])
        arrays[f"in_{name}"] = a
        args.append(nc.dram_tensor(f"in_{name}", a.shape, _mybir.dt.from_np(a.dtype), kind="ExternalInput").ap())
    args.append(nc.dram_tensor("out_0", (BATCHES, TOKENS, DIM), _mybir.dt.float32, kind="ExternalOutput").ap())
    build(nc, *args)
    r = _run(nc, [arrays], core_ids=[0])
    return r.results[0]["out_0"]
```

```python
from contextlib import ExitStack

import concourse.bass as bass
from concourse import mybir

F32 = mybir.dt.float32
F16 = mybir.dt.float16
BF16 = mybir.dt.bfloat16
I32 = mybir.dt.int32
ALU = mybir.AluOpType
ACT = mybir.ActivationFunctionType
AX_X = mybir.AxisListType.X
RMAX = bass.bass_isa.ReduceOp.max

P = 128
BATCHES = 16
TOKENS = 1024
DIM = 256
HIDDEN = 768
HEADS = 16
HEAD_DIM = DIM // HEADS
TILES = TOKENS // P
CHUNKS = DIM // P
HCHUNKS = HIDDEN // P
HALF = 512
HALVES = TOKENS // HALF
TPH = TILES // HALVES
GROUP = 4
GROUPS = HEADS // GROUP
CHEADS = P // HEAD_DIM
VW = 2 * HEAD_DIM
VPAIR = 3 * HEAD_DIM
EPS = 1e-5
SCORE_SCALE = 1.0 / 16.0
SCORE_BOUND = 70.0
V_BOUND = 2.0 ** 16
NORM_MARGIN = 1.02
NORM_LIMIT = (SCORE_BOUND / SCORE_SCALE) ** 2
W_SCALE = 1.0 / 127.0
W_EXACT = 256.0
H_SCALE = 2.0 ** 14 / (2.0 * 256.0 * 256.0)

Q_PARTS = (0, 0, 0, 1, 1, 2)
K_PARTS = (0, 1, 2, 0, 1, 0)
ROWS = len(Q_PARTS) * HEAD_DIM
SHIFT_ROWS = 3

UNITS = HEADS * TILES
STEPS = GROUPS * TILES
PREPARE = 4

QK = 8
PLACES = 2 * STEPS
NEXT_ITEMS = ([(4 * j, 4 * j + 2, "qk", j) for j in range(QK)] + [(40 + j, 40 + j, "norm", j) for j in range(QK)]
              + [(PLACES, PLACES, kind, j) for kind in ("v", "next xT") for j in range(4)])
OUT_ITEMS = [(56 + 2 * j, 57 + 2 * j, "out", j) for j in range(4)]
FIRST = [(-1, -1, "xT", j) for j in range(4)] + NEXT_ITEMS
ITEMS = sorted(NEXT_ITEMS + OUT_ITEMS, key=lambda item: item[0])
LAST_ITEMS = OUT_ITEMS
ON_SCALAR = ("xT", "next xT", "v")
FIRST_ACT = sum(item[2] in ON_SCALAR for item in FIRST)
ITEMS_ACT = sum(item[2] in ON_SCALAR for item in ITEMS)
DECIDE = 24
RELOAD = 28


def base(b):
    return len(FIRST) + len(ITEMS) * b


def freed(b):
    return len(FIRST) - FIRST_ACT + (len(ITEMS) - ITEMS_ACT) * b


def copied(b):
    return FIRST_ACT + ITEMS_ACT * b


def rank(items, at):
    return sum((item[2] in ON_SCALAR) == (items[at][2] in ON_SCALAR) for item in items[:at + 1])


def taken(items, step):
    return [n for n, item in enumerate(items) if item[1] in (2 * step, 2 * step + 1)]


def place(items, kind, n):
    return [item[2:] for item in items].index((kind, n))


def before(items, step):
    return sum(item[0] < 2 * step and item[2] not in ON_SCALAR for item in items)


EARLY = 4
POST_FILLS = ([("out", j) for j in range(4)] + [("x1T", 0), ("x1T", 1)]
              + [(w, g) for g in range(EARLY) for w in ("gate", "up")] + [("x1T", 2), ("x1T", 3)]
              + [(w, g) for g in range(EARLY, 2 * HCHUNKS) for w in ("gate", "up")] + [("down", j) for j in range(4)])
POST = len(POST_FILLS)
AT = {what: f for f, what in enumerate(POST_FILLS)}

LOADS = 2 * len(Q_PARTS)
GEN_FILL = GROUP * TILES * HALVES + 1
GEN_FREE = GROUP * TILES * HALVES + 3


def build(nc, x, Wq, bq, Wk, bk, Wv, bv, Wo, bo, w_gate, w_up, w_down, out):
    ctx = ExitStack()
    with ctx:
        def sb(name, shape, dt=F32):
            return ctx.enter_context(nc.sbuf_tensor(name, shape, dt))

        def sem(name):
            return ctx.enter_context(nc.semaphore(name))

        qstack = sb("qstack", [ROWS + SHIFT_ROWS, 2, GROUP, TOKENS], BF16)
        kstack = sb("kstack", [ROWS + SHIFT_ROWS, 2, GROUP, TOKENS], BF16)
        probs = sb("probs", [P, 2, GROUP, TOKENS])
        v = sb("v", [P, TILES, HEADS // 2, VPAIR])
        x_pre = sb("x_pre", [P, TILES, DIM])
        x_res = sb("x_res", [P, TILES, DIM])
        xT = sb("xT", [P, CHUNKS, TOKENS])
        parts = sb("parts", [P, 2, 3, TOKENS], BF16)
        rest = sb("rest", [P, 2, HALF])
        squares = sb("squares", [P, 4, TOKENS], BF16)
        pv = sb("pv", [P, HALVES, HALF])
        inv = sb("inv", [P, HALVES, HALF])
        outT = sb("outT", [P, CHUNKS, TOKENS])
        h32 = sb("h32", [P, 2, HALF])
        WqT = sb("WqT", [P, CHUNKS, DIM])
        WkT = sb("WkT", [P, CHUNKS, DIM])
        WvT = sb("WvT", [P, CHUNKS, DIM])
        WoT = sb("WoT", [P, CHUNKS, DIM])
        gateT = sb("gateT", [P, 3, CHUNKS * HIDDEN], BF16)
        upT = sb("upT", [P, 3, CHUNKS * HIDDEN], BF16)
        downT = sb("downT", [P, 3, HCHUNKS * DIM], BF16)
        bqk = sb("bqk", [P, 4])
        bv_col = sb("bv_col", [P, CHUNKS])
        bo_all = sb("bo_all", [P, DIM])
        ident = sb("ident", [P, P])
        blocks = sb("blocks", [P, P], BF16)
        norms = sb("norms", [P, QK])
        norm2 = sb("norm2", [P, 3])
        norm2_safe = sb("norm2_safe", [P, 3])
        norm2_all = sb("norm2_all", [P, 3])
        over = sb("over", [P, 2])
        wv_max = sb("wv_max", [P, 1])
        wv_max_all = sb("wv_max_all", [P, 1])
        flag = sb("flag", [P, 1], I32)
        halfmax = sb("halfmax", [P, GROUP * TILES * HALVES])
        rowmax = sb("rowmax", [P, P])
        shift = sb("shift", [P, 2, P])
        shift_parts = sb("shift_parts", [GROUP * TILES, SHIFT_ROWS, P], BF16)
        stats = sb("stats", [P, TILES, 6])
        meanvar = sb("meanvar", [P, TILES, 2])
        vareps = sb("vareps", [P, TILES])
        rstd = sb("rstd", [P, TILES])
        minus_half = sb("minus_half", [P, TILES])
        block_sums = sb("block_sums", [P, CHEADS])
        keep = sb("keep", [P, 2])
        neg_mean = sb("neg_mean", [P, TILES])
        ln_bias = sb("ln_bias", [P, TILES])
        margin = sb("margin", [P, 3])
        wmax = sb("wmax", [P, 3])
        wmax_all = sb("wmax_all", [P, 3])
        wtmp = sb("wtmp", [P, 3])
        h_scale = sb("h_scale", [P, 1])
        down_scale = sb("down_scale", [P, 1])
        wide = sb("wide", [P, 1], I32)

        flat = probs[:, :, :, :].rearrange("p a g n -> p (a g n)")
        H = HCHUNKS * HALF
        flat16 = flat.bitcast(F16)
        hT = [[flat16[:, (2 * s + i) * H:(2 * s + i + 1) * H].rearrange("p (c n) -> p c n", c=HCHUNKS)
               for i in range(2)] for s in range(HALVES)]
        tanh_out = [flat[:, 2 * H + s * HALF:2 * H + (s + 1) * HALF] for s in range(2)]
        gated = [flat[:, 2 * H + (2 + s) * HALF:2 * H + (3 + s) * HALF] for s in range(2)]
        out16 = outT[:, :, :].rearrange("p g n -> p (g n)").bitcast(F16)
        x1T = [out16[:, i * CHUNKS * TOKENS:(i + 1) * CHUNKS * TOKENS].rearrange("p (c n) -> p c n", c=CHUNKS)
               for i in range(2)]
        w4_raw = flat[:, 0:2048].rearrange("p (w c n) -> p w c n", w=4, c=CHUNKS)
        ints = flat[:, 2048:2048 + 3 * 1536]
        gate_raw = flat[:, 2048:3584].rearrange("p (c n) -> p c n", c=HCHUNKS)
        up_raw = flat[:, 3584:5120].rearrange("p (c n) -> p c n", c=HCHUNKS)
        down_raw = flat[:, 5120:6656].rearrange("p (c n) -> p c n", c=CHUNKS)
        w_rest = flat[:, 7168:7680]

        psum = ctx.enter_context(nc.psum_tensor("psum", [P, 8, HALF], F32))
        bank = [psum[:, i, :] for i in range(8)]
        scores = [psum[:, 2 * s:2 * s + 2, :] for s in range(2)]
        ACC, RING = 4, 6

        parts_dram = nc.dram_tensor("parts_dram", (BATCHES, 4, 3, P, TOKENS), BF16, kind="Internal").ap()

        bv_spread, wo_bv_made, bo_ready = sem("bv_spread"), sem("wo_bv_made"), sem("bo_ready")
        weights_loaded, ints_loaded, biases_loaded = sem("weights_loaded"), sem("ints_loaded"), sem("biases_loaded")
        wv_max_ready, wv_max_reduced = sem("wv_max_ready"), sem("wv_max_reduced")
        wmax_ready, wmax_reduced, wide_ready = sem("wmax_ready"), sem("wmax_reduced"), sem("wide_ready")
        consts_ready = sem("consts_ready")
        pool_step, dve_step = sem("pool_step"), sem("dve_step")
        setup_fill, setup_free = sem("setup_fill"), sem("setup_free")
        x_pre_loaded, x_res_loaded, x_res_biased = sem("x_pre_loaded"), sem("x_res_loaded"), sem("x_res_biased")
        work_fill, work_free, act_free = sem("work_fill"), sem("work_free"), sem("act_free")
        hi_ready, mid_ready, lo_ready, squares_ready = sem("hi_ready"), sem("mid_ready"), sem("lo_ready"), sem("squares_ready")
        parts_stored = [sem("parts_stored0"), sem("parts_stored1")]
        stack_loaded = [sem("stack_loaded0"), sem("stack_loaded1")]
        norm2_ready, norm2_reduced, flag_ready = sem("norm2_ready"), sem("norm2_reduced"), sem("flag_ready")
        gen_fill, gen_free = sem("gen_fill"), sem("gen_free")
        shift_ready, shift_loaded = sem("shift_ready"), sem("shift_loaded")
        scores_ready, probs_ready, pv_done = sem("scores_ready"), sem("probs_ready"), sem("pv_done")
        acc_free, out_ready = sem("acc_free"), sem("out_ready")
        post_fill, post_free = sem("post_fill"), sem("post_free")
        x1_hi_ready, tanh_ready, h_hi_ready, h_lo_ready = sem("x1_hi_ready"), sem("tanh_ready"), sem("h_hi_ready"), sem("h_lo_ready")
        stats_ready, rstd_ready, x1_ready, y_ready = sem("stats_ready"), sem("rstd_ready"), sem("x1_ready"), sem("y_ready")
        out_stored = sem("out_stored")

        x_v = x.rearrange("b (p t) d -> b p t d", t=TILES)
        out_v = out.rearrange("b (p t) d -> b p t d", t=TILES)

        block = ctx.enter_context(nc.Block())

        @block.sync
        def _(sp):
            for n, w in enumerate((Wq, Wk, Wv, Wo)):
                sp.dma_start(w4_raw[:, n, :, :], w.rearrange("(c p) k -> p c k", p=P)).then_inc(weights_loaded, 16)
            sp.dma_start(x_pre[:, :, :], x_v[0]).then_inc(x_pre_loaded, 16)
            with nc.allow_non_contiguous_dma(reason="three bias vectors, once"):
                sp.dma_start(bqk[:, 0:2], bq.rearrange("(c p) -> p c", p=P)).then_inc(biases_loaded, 16)
                sp.dma_start(bv_col[:, :], bv.rearrange("(c p) -> p c", p=P)).then_inc(biases_loaded, 16)
                sp.dma_start(bqk[:, 2:4], bk.rearrange("(c p) -> p c", p=P)).then_inc(biases_loaded, 16)
            sp.dma_start(bo_all[:, :], bo.partition_broadcast(P)).then_inc(biases_loaded, 16)
            for dst, w in ((gate_raw, w_gate), (up_raw, w_up), (down_raw, w_down)):
                sp.dma_start(dst.bitcast(I32), w.rearrange("(c p) k -> p c k", p=P)).then_inc(ints_loaded, 16)

            def store_parts(b, idx):
                sp.wait_ge(lo_ready, QK * b + 2 * idx + 2)
                sp.wait_ge(squares_ready, QK * b + 2 * idx + 2)
                sp.dma_start(parts_dram[b, idx].rearrange("j p n -> p j n"), parts[:, idx % 2, :, :]
                             ).then_inc(parts_stored[idx % 2], 16)

            def load_stack(b, g):
                slot, c, odd = g % 2, g // 2, g % 2
                for t, (stack, which) in enumerate(((qstack, Q_PARTS), (kstack, K_PARTS))):
                    src = parts_dram[b, 2 * t + c]
                    for r, part in enumerate(which):
                        sp.dma_start(stack[r * HEAD_DIM:(r + 1) * HEAD_DIM, slot, :, :],
                                     src[part].rearrange("(h d) n -> d h n", d=HEAD_DIM)[:, odd::2, :]
                                     ).then_inc(stack_loaded[slot], 16)

            def load_shift(b, g):
                sp.wait_ge(shift_ready, GROUPS * b + g + 1)
                for r in range(SHIFT_ROWS):
                    sp.dma_start(kstack[ROWS + r:ROWS + r + 1, g % 2, :, :].rearrange("o h (t n) -> o (h t) n", t=TILES),
                                 shift_parts[:, r, :]).then_inc(shift_loaded, 16)

            sp.wait_ge(work_fill, place(FIRST, "xT", 3) + 1)
            sp.dma_start(x_pre[:, :, :], x_v[1]).then_inc(x_pre_loaded, 16)
            for idx in range(4):
                store_parts(0, idx)
            for s in range(2):
                sp.wait_ge(parts_stored[s], 32)
            load_stack(0, 0)
            load_shift(0, 0)
            load_stack(0, 1)

            def store_result(b):
                for s in range(2):
                    sp.wait_ge(y_ready, 4 * b + 2 * (s + 1))
                    sp.dma_start(out_v[b][:, TPH * s:TPH * (s + 1), :], x_res[:, TPH * s:TPH * (s + 1), :]
                                 ).then_inc(out_stored, 16)

            def batch(b, first, last, ahead=2):
                if not last:
                    sp.wait_ge(work_fill, base(b))
                    sp.dma_start(x_pre[:, :, :], x_v[ahead - 1:BATCHES][b + 1]).then_inc(x_pre_loaded, 16)
                if not first:
                    store_result(b - 1)
                    sp.wait_ge(out_stored, 32 * b)
                sp.dma_start(x_res[:, :, :], x_v[b]).then_inc(x_res_loaded, 16)
                if not last:
                    store_parts(b + 1, 0)
                load_shift(b, 1)
                if not last:
                    store_parts(b + 1, 1)
                sp.wait_ge(scores_ready, UNITS * b + GROUP * TILES)
                load_stack(b, 2)
                if not last:
                    store_parts(b + 1, 2)
                load_shift(b, 2)
                sp.wait_ge(scores_ready, UNITS * b + 2 * GROUP * TILES)
                load_stack(b, 3)
                if not last:
                    store_parts(b + 1, 3)
                load_shift(b, 3)
                if not last:
                    sp.wait_ge(scores_ready, UNITS * b + 3 * GROUP * TILES)
                    for s in range(2):
                        sp.wait_ge(parts_stored[s], 32 * (b + 2))
                    load_stack(b + 1, 0)
                    load_shift(b + 1, 0)
                    sp.wait_ge(scores_ready, UNITS * (b + 1))
                    load_stack(b + 1, 1)

            batch(0, True, False)
            with sp.Fori(1, BATCHES - 2) as b:
                batch(b, False, False)
            batch(BATCHES - 2, False, False, ahead=1)
            batch(BATCHES - 1, False, True)
            store_result(BATCHES - 1)
            sp.wait_ge(out_stored, 32 * BATCHES)

        @block.gpsimd
        def _(pool):
            step = 0

            def then(ins):
                nonlocal step
                step += 1
                ins.then_inc(pool_step, 1)
                pool.wait_ge(pool_step, step)

            then(nc.gpsimd.memset(ident[:, :], 0.0))
            nc.gpsimd.affine_select(out=ident[:, :], in_=ident[:, :], compare_op=ALU.not_equal, fill=1.0, base=0,
                                    pattern=[[-1, P]], channel_multiplier=1).then_inc(consts_ready, 1)
            then(nc.gpsimd.memset(blocks[:, :], 1.0))
            blk = blocks[:, :].rearrange("p (h d) -> p h d", d=HEAD_DIM)
            then(nc.gpsimd.affine_select(out=blk, in_=blk, compare_op=ALU.is_ge, fill=0.0, base=0,
                                         pattern=[[-HEAD_DIM, CHEADS], [0, HEAD_DIM]], channel_multiplier=1))
            nc.gpsimd.affine_select(out=blk, in_=blk, compare_op=ALU.is_ge, fill=0.0, base=HEAD_DIM - 1,
                                    pattern=[[HEAD_DIM, CHEADS], [0, HEAD_DIM]], channel_multiplier=-1
                                    ).then_inc(consts_ready, 1)
            nc.gpsimd.memset(v[:, :, :, HEAD_DIM:2 * HEAD_DIM], 1.0).then_inc(consts_ready, 1)
            then(nc.gpsimd.memset(minus_half[:, :], -0.5))
            then(nc.gpsimd.memset(margin[:, :], NORM_MARGIN))
            pool.wait_ge(wv_max_ready, 1)
            nc.gpsimd.partition_all_reduce(wv_max_all[:, :], wv_max[:, :], P, RMAX).then_inc(wv_max_reduced, 1)
            setup_steps = step

            def split(b, items, start):
                for j in range(QK):
                    s, idx, hf = j % 2, j // 2, j % 2
                    cols = slice(hf * HALF, (hf + 1) * HALF)
                    pool.wait_ge(work_free, start + rank(items, place(items, "qk", j)))
                    nc.gpsimd.tensor_tensor(squares[:, idx, cols], parts[:, idx % 2, 0, cols],
                                            parts[:, idx % 2, 0, cols], ALU.mult).then_inc(squares_ready, 1)
                    nc.gpsimd.tensor_copy(parts[:, idx % 2, 1, cols], rest[:, s, :]).then_inc(mid_ready, 1)
                    pool.wait_ge(mid_ready, QK * b + j + 1)
                    nc.gpsimd.tensor_tensor(parts[:, idx % 2, 2, cols], rest[:, s, :], parts[:, idx % 2, 1, cols],
                                            ALU.subtract).then_inc(lo_ready, 1)
                pool.wait_ge(norm2_ready, b + 1)
                nc.gpsimd.tensor_tensor(norm2_safe[:, :], norm2[:, :], margin[:, :], ALU.mult)
                pool.drain()
                nc.gpsimd.partition_all_reduce(norm2_all[:, :], norm2_safe[:, :], P, RMAX).then_inc(norm2_reduced, 1)

            def make_rstd(b, j, which):
                tiles = slice(2 * j, 2 * j + 2)
                n = TILES * b + 4 * which + j
                pool.wait_ge(stats_ready, n + 1)
                nc.gpsimd.tensor_tensor(rstd[:, tiles], vareps[:, tiles], minus_half[:, tiles], ALU.pow
                                        ).then_inc(pool_step, 1)
                pool.wait_ge(pool_step, n + 1 + setup_steps)
                nc.gpsimd.tensor_tensor(ln_bias[:, tiles], neg_mean[:, tiles], rstd[:, tiles], ALU.mult
                                        ).then_inc(rstd_ready, 1)

            def batch(b, last):
                pool.wait_ge(x_res_loaded, 16 * (b + 1))
                nc.gpsimd.tensor_tensor(x_res[:, :, :], x_res[:, :, :],
                                        bo_all[:, :].unsqueeze(1).to_broadcast([P, TILES, DIM]), ALU.add
                                        ).then_inc(x_res_biased, 1)
                if not last:
                    split(b + 1, ITEMS, freed(b))
                for j in range(4):
                    make_rstd(b, j, 0)
                for g in range(2 * HCHUNKS):
                    hf, hc = g // HCHUNKS, g % HCHUNKS
                    pool.wait_ge(h_hi_ready, 2 * HCHUNKS * b + g + 1)
                    nc.gpsimd.tensor_tensor(hT[hf][1][:, hc, :], h32[:, g % 2, :], hT[hf][0][:, hc, :], ALU.subtract
                                            ).then_inc(h_lo_ready, 1)
                for j in range(4):
                    make_rstd(b, j, 1)

            split(0, FIRST, 0)
            pool.wait_ge(wmax_ready, 1)
            nc.gpsimd.partition_all_reduce(wmax_all[:, :], wmax[:, :], P, RMAX).then_inc(wmax_reduced, 1)
            pool.wait_ge(bo_ready, 1)
            batch(0, False)
            with pool.Fori(1, BATCHES - 1) as b:
                batch(b, False)
            batch(BATCHES - 1, True)

        @block.scalar
        def _(act):
            act.wait_ge(biases_loaded, 64)

            def hi(b, j, start, at, first):
                idx, hf = j // 2, j % 2
                act.wait_ge(work_fill, start + at + 1)
                if hf == 0 and not (first and idx < 2):
                    act.wait_ge(parts_stored[idx % 2], 32 * b + 16 * (idx // 2))
                nc.scalar.activation(parts[:, idx % 2, 0, hf * HALF:(hf + 1) * HALF], bank[RING + at % 2],
                                     ACT.Identity, bias=bqk[:, idx:idx + 1]).then_inc(hi_ready, 1)

            def copy_v(j, start, at):
                act.wait_ge(work_fill, start + at + 1)
                vt = v[:, 2 * j:2 * j + 2, :, :].rearrange("p t r (e d) -> p (t r) e d", d=HEAD_DIM)
                nc.scalar.activation(vt[:, :, 0::2, :],
                                     bank[RING + at % 2].rearrange("p (r e d) -> p r e d", e=2, d=HEAD_DIM), ACT.Copy
                                     ).then_inc(act_free, 1)

            def normalise(b, j, which, done):
                act.wait_ge(rstd_ready, TILES * b + 4 * which + j + 1)
                for t in (2 * j, 2 * j + 1):
                    ins = nc.scalar.activation(x_res[:, t, :], x_res[:, t, :], ACT.Identity,
                                               scale=rstd[:, t:t + 1], bias=ln_bias[:, t:t + 1])
                ins.then_inc(done, 1)

            def copy_xT(j, start, at):
                hf, c = j // 2, j % 2
                act.wait_ge(work_fill, start + at + 1)
                nc.scalar.activation(xT[:, c, hf * HALF:(hf + 1) * HALF], bank[RING + at % 2], ACT.Copy
                                     ).then_inc(act_free, 1)

            def attention(b, first, last):
                for u in range(UNITS):
                    k, h = u // GROUP, u % GROUP
                    if u == GROUP and not first:
                        act.wait_ge(post_free, POST * b)
                    act.wait_ge(scores_ready, UNITS * b + u + 1)
                    if h == 0 and k >= 2:
                        act.wait_ge(pv_done, 2 * STEPS * b + 2 * (k - 1))
                    nc.scalar.activation(probs[:, k % 2, h, :], scores[u % 2].rearrange("p a n -> p (a n)"), ACT.Exp,
                                         scale=SCORE_SCALE).then_inc(probs_ready, 1)
                    if u == GROUP - 1 and not first:
                        normalise(b - 1, 3, 1, y_ready)
                    if h == 0 and not last:
                        for n in taken(ITEMS, k - 1):
                            if ITEMS[n][2] == "qk":
                                hi(b + 1, ITEMS[n][3], base(b), n, False)
                if not last:
                    act.wait_ge(pv_done, 2 * STEPS * (b + 1))
                    for j in range(4):
                        copy_v(j, base(b), place(ITEMS, "v", j))

            def post(b, last):
                def x1_hi(n):
                    f, hf, c = AT["x1T", n], n // 2, n % 2
                    act.wait_ge(post_fill, POST * b + f + 1)
                    nc.scalar.activation(x1T[0][:, c, hf * HALF:(hf + 1) * HALF], bank[f % 4], ACT.Copy
                                         ).then_inc(x1_hi_ready, 1)

                def tanh(g):
                    f = AT["gate", g]
                    act.wait_ge(post_fill, POST * b + f + 1)
                    if g >= 2:
                        act.wait_ge(post_free, POST * b + AT["gate", g - 2] + 1)
                    nc.scalar.activation(tanh_out[g % 2], bank[f % 4], ACT.Tanh, scale=0.5 * W_SCALE
                                         ).then_inc(tanh_ready, 1)

                def h_hi(g):
                    act.wait_ge(post_free, POST * b + AT["up", g] + 1)
                    nc.scalar.activation(hT[g // HCHUNKS][0][:, g % HCHUNKS, :], h32[:, g % 2, :], ACT.Copy
                                         ).then_inc(h_hi_ready, 1)

                for n in range(2):
                    normalise(b, n, 0, x1_ready)
                    if not last:
                        copy_xT(n, base(b), place(ITEMS, "next xT", n))
                for n in range(2):
                    x1_hi(n)
                if not last:
                    for j in range(2, 4):
                        copy_xT(j, base(b), place(ITEMS, "next xT", j))
                for n in range(2, 4):
                    normalise(b, n, 0, x1_ready)
                for g in range(2 * HCHUNKS):
                    tanh(g)
                    if g >= 1:
                        h_hi(g - 1)
                    if g == EARLY - 1:
                        for n in range(2, 4):
                            x1_hi(n)
                h_hi(2 * HCHUNKS - 1)
                for j in range(4 if last else 3):
                    normalise(b, j, 1, y_ready)

            for j in range(4):
                copy_xT(j, 0, place(FIRST, "xT", j))
            for j in range(QK):
                hi(0, j, 0, place(FIRST, "qk", j), True)
            for j in range(4):
                copy_v(j, 0, place(FIRST, "v", j))
            for j in range(4):
                copy_xT(j, 0, place(FIRST, "next xT", j))

            def batch(b, first, last):
                attention(b, first, last)
                post(b, last)

            batch(0, True, False)
            with act.Fori(1, BATCHES - 1) as b:
                batch(b, False, False)
            batch(BATCHES - 1, False, True)

        @block.vector
        def _(dve):
            steps = 0

            def then(ins):
                nonlocal steps
                steps += 1
                ins.then_inc(dve_step, 1)
                dve.wait_ge(dve_step, steps)

            nc.vector.memset(qstack[ROWS:ROWS + SHIFT_ROWS, :, :, :], 1.0).then_inc(consts_ready, 1)
            then(nc.vector.memset(rowmax[:, :], 0.0))
            for f, t in enumerate((WoT, WqT, WkT, WvT)):
                dve.wait_ge(setup_fill, f + 1)
                nc.vector.tensor_copy(t[:, :, :].rearrange("p c n -> p (c n)"), bank[f]).then_inc(setup_free, 1)
            dve.wait_ge(setup_free, 4)
            nc.vector.tensor_reduce(wv_max[:, :], WvT[:, :, :].rearrange("p c n -> p (c n)"), AX_X, ALU.max,
                                    apply_absolute_value=True).then_inc(wv_max_ready, 1)
            dve.wait_ge(biases_loaded, 64)
            dve.wait_ge(consts_ready, 4)
            for c in range(CHUNKS):
                ins = nc.vector.tensor_scalar(rest[:, 0, c * P:(c + 1) * P], ident[:, :], 0.0, bv_col[:, c:c + 1],
                                              ALU.mult, ALU.add)
            ins.then_inc(bv_spread, 1)
            then(nc.vector.tensor_reduce(block_sums[:, :], ident[:, :].rearrange("p (h d) -> p h d", d=HEAD_DIM), AX_X,
                                         ALU.add))
            for odd in range(2):
                nc.vector.tensor_reduce(keep[:, odd:odd + 1], block_sums[:, odd::2], AX_X, ALU.add)
            dve.wait_ge(wo_bv_made, 1)
            nc.vector.tensor_tensor(bo_all[:, :], bank[ACC][:, 0:DIM], bo_all[:, :], ALU.add).then_inc(bo_ready, 1)

            def take_work(b, kind, j, n, bank_of, first):
                o = bank[RING + bank_of]
                if kind == "qk":
                    idx, hf = j // 2, j % 2
                    dve.wait_ge(hi_ready, QK * b + j + 1)
                    if j >= 2 or not first:
                        dve.wait_ge(lo_ready, QK * b + j - 1)
                    nc.vector.scalar_tensor_tensor(out=rest[:, j % 2, :], in0=o, scalar=bqk[:, idx:idx + 1],
                                                   in1=parts[:, idx % 2, 0, hf * HALF:(hf + 1) * HALF],
                                                   op0=ALU.add, op1=ALU.subtract).then_inc(work_free, 1)
                elif kind == "norm":
                    if j == 0:
                        dve.wait_ge(act_free, 4 if first else copied(b - 1))
                        nc.vector.tensor_reduce(norm2[:, 2:3], xT[:, :, :].rearrange("p c n -> p (c n)"), AX_X,
                                                ALU.max, apply_absolute_value=True)
                    dve.wait_ge(work_fill, n + 1)
                    nc.vector.tensor_reduce(norms[:, j:j + 1], o, AX_X, ALU.max).then_inc(work_free, 1)
                    if j == QK - 1:
                        dve.drain()
                        nc.vector.tensor_reduce(norm2[:, 0:2], norms[:, :].rearrange("p (t j) -> p t j", t=2), AX_X,
                                                ALU.max).then_inc(norm2_ready, 1)
                elif kind == "out":
                    if j == 0:
                        dve.wait_ge(x_res_biased, b + 1)
                    dve.wait_ge(work_fill, n + 1)
                    i = 2 * j
                    tiles = x_res[:, i:i + 2, :].rearrange("p t d -> p (t d)")
                    nc.vector.tensor_tensor(tiles, o, tiles, ALU.add).then_inc(work_free, 1)

            def decide(b):
                dve.wait_ge(norm2_reduced, b + 1)
                nc.vector.tensor_scalar(over[:, 0:1], norm2_all[:, 0:1], norm2_all[:, 1:2], NORM_LIMIT, ALU.mult,
                                        ALU.is_ge)
                nc.vector.tensor_scalar(over[:, 1:2], norm2_all[:, 2:3], wv_max_all[:, :], V_BOUND / DIM, ALU.mult,
                                        ALU.is_ge)
                dve.drain()
                nc.vector.tensor_tensor(flag[:, :], over[:, 0:1], over[:, 1:2], ALU.max).then_inc(flag_ready, 1)

            general = dve.alloc_register("dve_general")

            def prepare_shift(n, first=False):
                with dve.If_eq(general, 1):
                    dve.sem_inc(gen_free, 2)
                    with dve.Fori(0, GROUP) as h:
                        for w in range(TILES * HALVES):
                            dve.wait_ge(gen_fill, GEN_FILL * n + TILES * HALVES * h + w + 1)
                            nc.vector.tensor_reduce(halfmax[:, bass.ds(TILES * HALVES * h + w, 1)], bank[RING + w % 2],
                                                    AX_X, ALU.max).then_inc(gen_free, 1)
                    dve.drain()
                    nc.vector.tensor_reduce(rowmax[:, 0:GROUP * TILES],
                                            halfmax[:, :].rearrange("p (n f) -> p n f", f=HALVES), AX_X, ALU.max
                                            ).then_inc(gen_free, 1)
                    R = GROUP * TILES
                    dve.wait_ge(gen_fill, GEN_FILL * (n + 1))
                    nc.vector.tensor_scalar(shift[0:R, 0, :], bank[RING][0:R, 0:P], -1.0, None, ALU.mult)
                    dve.drain()
                    if not first:
                        dve.wait_ge(shift_loaded, 16 * SHIFT_ROWS * n)
                    nc.vector.tensor_copy(shift_parts[:, 0, :], shift[0:R, 0, :])
                    dve.drain()
                    nc.vector.tensor_tensor(shift[0:R, 1, :], shift[0:R, 0, :], shift_parts[:, 0, :], ALU.subtract)
                    dve.drain()
                    nc.vector.tensor_copy(shift_parts[:, 1, :], shift[0:R, 1, :])
                    dve.drain()
                    nc.vector.tensor_tensor(shift_parts[:, 2, :], shift[0:R, 1, :], shift_parts[:, 1, :],
                                            ALU.subtract).then_inc(shift_ready, 1)
                with dve.Else():
                    dve.sem_inc(gen_free, GEN_FREE)
                    if not first:
                        dve.wait_ge(shift_loaded, 16 * SHIFT_ROWS * n)
                    nc.vector.memset(shift_parts[:, :, :], 0.0).then_inc(shift_ready, 1)

            def take_group(b, g):
                c, odd = g // 2, g % 2
                from_sums = [(1 - odd) * HEAD_DIM + i % HEAD_DIM for i in range(VW)]
                done = 2 * STEPS * b + 2 * (TILES * (g + 1) - 1)
                keep_v, keep_sums = keep[:, odd:odd + 1], keep[:, 1 - odd:2 - odd]
                tail = g == GROUPS - 1
                if tail:
                    src = [bank[ACC + hf] for hf in range(HALVES)]
                else:
                    src = [pv[:, hf, :] for hf in range(HALVES)]
                    for hf in range(HALVES):
                        dve.wait_ge(pv_done, done + hf + 1)
                        nc.vector.tensor_copy(src[hf], bank[ACC + hf]).then_inc(acc_free, 1)
                    dve.drain()
                if tail:
                    dve.wait_ge(pv_done, done + 1)
                    nc.vector.tensor_copy(pv[:, 0, 0:1], src[0][:, 0:1])
                nc.vector.stream_shuffle(inv[:, 0, :], src[0], from_sums)
                if tail:
                    dve.wait_ge(pv_done, done + 2)
                nc.vector.tensor_scalar(inv[:, 1, :], src[1], keep_sums, None, ALU.mult)
                dve.drain()
                nc.vector.scalar_tensor_tensor(out=inv[:, 0, :], in0=inv[:, 0, :], scalar=keep_v, in1=inv[:, 1, :],
                                               op0=ALU.mult, op1=ALU.add)
                dve.drain()
                nc.vector.reciprocal(inv[:, 0, :], inv[:, 0, :])
                dve.drain()
                for hf in range(HALVES):
                    if hf == 1:
                        nc.vector.stream_shuffle(inv[:, 1, :], inv[:, 0, :], from_sums)
                        dve.drain()
                    half = outT[:, c, hf * HALF:(hf + 1) * HALF]
                    ins = nc.vector.scalar_tensor_tensor(out=pv[:, hf, :] if odd else half, in0=src[hf], scalar=keep_v,
                                                         in1=inv[:, hf, :], op0=ALU.mult, op1=ALU.mult)
                    if tail:
                        ins.then_inc(acc_free, 1)
                    if odd:
                        dve.drain()
                        ins = nc.vector.tensor_tensor(half, pv[:, hf, :], half, ALU.add)
                    ins.then_inc(out_ready, 1)

            def add(b, what, j, scale):
                f = AT[what, j]
                tiles = x_res[:, 2 * j:2 * j + 2, :].rearrange("p t d -> p (t d)")
                dve.wait_ge(post_fill, POST * b + f + 1)
                nc.vector.scalar_tensor_tensor(out=tiles, in0=bank[f % 4], scalar=scale, in1=tiles, op0=ALU.mult,
                                               op1=ALU.add).then_inc(post_free, 1)

            def find_stats(b, what, j):
                dve.wait_ge(post_free, POST * b + AT[what, j] + 1)
                for i in range(2):
                    nc.vector.bn_stats(stats[:, 2 * j + i, :], x_res[:, 2 * j + i, :])
                dve.drain()
                for i in range(2):
                    nc.vector.bn_aggr(meanvar[:, 2 * j + i, :], stats[:, 2 * j + i, :])
                dve.drain()
                tiles = slice(2 * j, 2 * j + 2)
                nc.vector.tensor_scalar(vareps[:, tiles], meanvar[:, tiles, 1], EPS, None, ALU.add)
                nc.vector.tensor_scalar(neg_mean[:, tiles], meanvar[:, tiles, 0], -1.0, None, ALU.mult
                                        ).then_inc(stats_ready, 1)

            def post(b):
                def x1_lo(n):
                    f, hf, c = AT["x1T", n], n // 2, n % 2
                    dve.wait_ge(x1_hi_ready, 4 * b + n + 1)
                    cols = slice(hf * HALF, (hf + 1) * HALF)
                    nc.vector.tensor_tensor(x1T[1][:, c, cols], bank[f % 4], x1T[0][:, c, cols], ALU.subtract
                                            ).then_inc(post_free, 1)

                def gate(g):
                    f = AT["gate", g]
                    dve.wait_ge(tanh_ready, 2 * HCHUNKS * b + g + 1)
                    nc.vector.scalar_tensor_tensor(out=gated[g % 2], in0=tanh_out[g % 2], scalar=1.0, in1=bank[f % 4],
                                                   op0=ALU.add, op1=ALU.mult).then_inc(post_free, 1)
                    dve.wait_ge(post_fill, POST * b + f + 2)
                    dve.wait_ge(post_free, POST * b + f + 1)
                    if g >= 2:
                        dve.wait_ge(h_lo_ready, 2 * HCHUNKS * b + g - 1)
                    nc.vector.scalar_tensor_tensor(out=h32[:, g % 2, :], in0=gated[g % 2], scalar=h_scale[:, 0:1],
                                                   in1=bank[(f + 1) % 4], op0=ALU.mult, op1=ALU.mult
                                                   ).then_inc(post_free, 1)

                for j in range(2):
                    add(b, "out", j, 1.0)
                    find_stats(b, "out", j)
                add(b, "out", 2, 1.0)
                add(b, "out", 3, 1.0)
                find_stats(b, "out", 2)
                x1_lo(0)
                x1_lo(1)
                find_stats(b, "out", 3)
                for g in range(2 * HCHUNKS):
                    gate(g)
                    if g == EARLY - 1:
                        x1_lo(2)
                        x1_lo(3)
                for j in range(4):
                    add(b, "down", j, down_scale[:, 0:1])
                    find_stats(b, "down", j)

            def batch(b, first, last):
                items = LAST_ITEMS if last else ITEMS

                def take_items(step):
                    for n in taken(items, step):
                        kind, j = items[n][2:]
                        take_work(b if kind == "out" else b + 1, kind, j, base(b) + n, n % 2, False)

                for k in range(STEPS):
                    if k == DECIDE and not last:
                        decide(b + 1)
                        dve.wait_ge(flag_ready, b + 2)
                    if k % TILES == 0 and k:
                        take_group(b, k // TILES - 1)
                    if k == RELOAD and not last:
                        dve.reg_load(general, flag[0:1, 0:1])
                    if k % TILES == PREPARE and not (last and k // TILES == GROUPS - 1):
                        prepare_shift(GROUPS * b + k // TILES + 1)
                    take_items(k)
                take_group(b, GROUPS - 1)
                post(b)

            for n, (_, _, kind, j) in enumerate(FIRST):
                take_work(0, kind, j, n, n % 2, True)
            dve.wait_ge(wv_max_reduced, 1)
            decide(0)
            dve.wait_ge(flag_ready, 1)
            dve.reg_load(general, flag[0:1, 0:1])
            prepare_shift(0, True)
            dve.wait_ge(ints_loaded, 48)
            then(nc.vector.tensor_copy(ints, ints.bitcast(I32)))
            nc.vector.tensor_reduce(wmax[:, :], ints.rearrange("p (w n) -> p w n", w=3), AX_X, ALU.max,
                                    apply_absolute_value=True).then_inc(wmax_ready, 1)
            dve.wait_ge(wmax_reduced, 1)
            then(nc.vector.tensor_scalar(wmax[:, :], wmax_all[:, :], 1.0, None, ALU.max))
            then(nc.vector.tensor_scalar(wtmp[:, 0:1], wmax[:, 0:1], wmax[:, 1:2], None, ALU.mult))
            then(nc.vector.reciprocal(wtmp[:, 1:2], wtmp[:, 0:1]))
            then(nc.vector.tensor_scalar(h_scale[:, :], wtmp[:, 1:2], H_SCALE, None, ALU.mult))
            then(nc.vector.tensor_scalar(down_scale[:, :], wtmp[:, 0:1], 0.5 * W_SCALE ** 3 / H_SCALE, None, ALU.mult))
            then(nc.vector.tensor_reduce(wtmp[:, 2:3], wmax[:, :], AX_X, ALU.max))
            nc.vector.tensor_scalar(wide[:, :], wtmp[:, 2:3], W_EXACT, None, ALU.is_gt).then_inc(wide_ready, 1)
            wide_weights = dve.alloc_register("dve_wide")
            dve.wait_ge(wide_ready, 1)
            dve.reg_load(wide_weights, wide[0:1, 0:1])

            def take_weights(w_parts):
                f = 4
                for t in (gateT, upT, downT):
                    for i in range(3):
                        cols = slice(i * HALF, (i + 1) * HALF)
                        dve.wait_ge(setup_fill, f + 1)
                        ins = nc.vector.tensor_copy(t[:, 0, cols], bank[f % 4])
                        if w_parts == 3:
                            dve.drain()
                            nc.vector.tensor_tensor(w_rest, bank[f % 4], t[:, 0, cols], ALU.subtract)
                            dve.drain()
                            nc.vector.tensor_copy(t[:, 1, cols], w_rest)
                            dve.drain()
                            ins = nc.vector.tensor_tensor(t[:, 2, cols], w_rest, t[:, 1, cols], ALU.subtract)
                        ins.then_inc(setup_free, 1)
                        f += 1

            with dve.If_eq(wide_weights, 1):
                take_weights(3)
            with dve.Else():
                take_weights(1)
            batch(0, True, False)
            with dve.Fori(1, BATCHES - 1) as b:
                batch(b, False, False)
            batch(BATCHES - 1, False, True)

        @block.tensor
        def _(pe):
            def mm(o, lhsT, rhs, start, stop):
                return nc.tensor.matmul(o, lhsT, rhs, start=start, stop=stop)

            def flip(o, src):
                return nc.tensor.transpose(o, src, ident[:, :])

            pe.wait_ge(consts_ready, 4)
            pe.wait_ge(weights_loaded, 16 * 4)
            tiles = []
            for n in (3, 0, 1, 2):
                tiles += [w4_raw[:, n, o, k * P:(k + 1) * P] for k in range(CHUNKS) for o in range(CHUNKS)]
            for raw in (gate_raw, up_raw):
                tiles += [raw[:, hc, k * P:(k + 1) * P] for k in range(CHUNKS) for hc in range(HCHUNKS)]
            tiles += [down_raw[:, c, hc * P:(hc + 1) * P] for hc in range(HCHUNKS) for c in range(CHUNKS)]
            fills = len(tiles) // 4

            def flip_weights(f):
                if f >= 4:
                    pe.wait_ge(setup_free, f - 3)
                for i in range(4):
                    ins = flip(bank[f % 4][:, i * P:(i + 1) * P], tiles[4 * f + i])
                ins.then_inc(setup_fill, 1)

            for f in range(4):
                flip_weights(f)
            pe.wait_ge(setup_free, 4)
            pe.wait_ge(bv_spread, 1)
            for c in range(CHUNKS):
                ins = mm(bank[ACC][:, 0:DIM], rest[:, 0, c * P:(c + 1) * P], WoT[:, c, :],
                         c == 0, c == CHUNKS - 1)
            ins.then_inc(wo_bv_made, 1)

            general = pe.alloc_register("pe_general")
            wide_weights = pe.alloc_register("pe_wide")

            def do_work(b, items, at, half=None):
                kind, j = items[at][2:]
                o = bank[RING + at % 2]
                if items is FIRST:
                    data, by_dve, by_act, xT_copied = int(kind == "next xT"), 0, 0, 4
                else:
                    data = b if kind == "out" else b + 1 if kind != "next xT" else b + 2
                    by_dve, by_act, xT_copied = freed(b), copied(b), copied(b)
                halves = range(2) if half is None else (half,)
                if half != 1:
                    if at >= 2 and items[at - 2][2] in ON_SCALAR:
                        pe.wait_ge(act_free, by_act + rank(items, at - 2))
                    elif at >= 2:
                        pe.wait_ge(work_free, by_dve + rank(items, at - 2))
                    elif items is not FIRST:
                        pe.wait_ge(act_free, by_act - 1 + at)
                if kind in ("xT", "next xT"):
                    hf, c = j // 2, j % 2
                    if j == 0 and half != 1:
                        pe.wait_ge(x_pre_loaded, 16 * (data + 1))
                    for i in [2 * m + i for m in halves for i in range(2)]:
                        ins = flip(o[:, i * P:(i + 1) * P], x_pre[:, hf * TPH + i, c * P:(c + 1) * P])
                elif kind == "qk":
                    idx, hf = j // 2, j % 2
                    w, c = (WqT, WkT)[idx // 2], idx % 2
                    if j == 0 and half != 1:
                        pe.wait_ge(act_free, xT_copied)
                    for k in halves:
                        ins = mm(o, w[:, k, c * P:(c + 1) * P], xT[:, k, hf * HALF:(hf + 1) * HALF],
                                 k == 0, k == CHUNKS - 1)
                elif kind == "norm":
                    if half != 1:
                        pe.wait_ge(squares_ready, QK * data + j + 1)
                        ins = mm(o, blocks[:, :], squares[:, j // 2, (j % 2) * HALF:(j % 2 + 1) * HALF], True, True)
                        ins.then_inc(work_fill, 1)
                    return
                elif kind == "v":
                    for i in halves:
                        t = 2 * j + i
                        for k in range(CHUNKS):
                            ins = mm(o[:, i * DIM:(i + 1) * DIM], xT[:, k, t * P:(t + 1) * P], WvT[:, k, :],
                                     k == 0, k == CHUNKS - 1)
                elif kind == "out":
                    ins = project(b, 0, j, o, halves)
                if half != 0:
                    ins.then_inc(work_fill, 1)

            def project(b, c, j, o, halves=range(2)):
                if j % 2 == 0 and 0 in halves:
                    pe.wait_ge(out_ready, 2 * GROUPS * b + 2 * (2 * c + 1) + j // 2 + 1)
                for i in halves:
                    t = 2 * j + i
                    ins = mm(o[:, i * DIM:(i + 1) * DIM], outT[:, c, t * P:(t + 1) * P], WoT[:, c, :], True, True)
                return ins

            def stack_here(n, slot, b, g):
                pe.wait_ge(stack_loaded[slot], 16 * LOADS * (2 * b + g // 2 + 1))

            def prepare_shift(n, b, g, work_done):
                slot = g % 2
                kflat = kstack[0:ROWS, slot, :, :].rearrange("r h n -> r (h n)")
                qflat = qstack[0:ROWS, slot, :, :].rearrange("r h n -> r (h n)")
                with pe.If_eq(general, 1):
                    with pe.Fori(0, GROUP) as h:
                        for w in range(TILES * HALVES):
                            t, hf = w // HALVES, w % HALVES
                            if w == 0:
                                stack_here(n, slot, b, g)
                                pe.wait_ge(work_free, work_done)
                            pe.wait_ge(gen_free, GEN_FREE * n + TILES * HALVES * h + w + 1)
                            mm(bank[RING + w % 2], kflat[:, bass.ds(TOKENS * h + P * t, P)],
                               qflat[:, bass.ds(TOKENS * h + HALF * hf, HALF)], True, True).then_inc(gen_fill, 1)
                    pe.wait_ge(gen_free, GEN_FREE * (n + 1))
                    flip(bank[RING][:, 0:P], rowmax[:, :]).then_inc(gen_fill, 1)
                    pe.wait_ge(shift_ready, n + 1)
                with pe.Else():
                    pe.sem_inc(gen_fill, GEN_FILL)

            def attention(b, first, last):
                items = LAST_ITEMS if last else ITEMS

                def do_items(at):
                    for n, item in enumerate(items):
                        if item[:2] == (at, at):
                            do_work(b, items, n)
                        elif at in item[:2]:
                            do_work(b, items, n, item.index(at))

                def score(u):
                    k, h = u // GROUP, u % GROUP
                    g, t = k // TILES, k % TILES
                    if t == 0 and h == 0:
                        stack_here(GROUPS * b + g, g % 2, b, g)
                        pe.wait_ge(shift_loaded, 16 * SHIFT_ROWS * (GROUPS * b + g + 1))
                    if u < 2 and not first:
                        pe.wait_ge(post_free, POST * b - 2 + 2 * u)
                    if u >= 2:
                        pe.wait_ge(probs_ready, UNITS * b + u - 1)
                    for hf in range(HALVES):
                        ins = mm(scores[u % 2][:, hf, :], qstack[:, g % 2, h, t * P:(t + 1) * P],
                                 kstack[:, g % 2, h, hf * HALF:(hf + 1) * HALF], True, True)
                    ins.then_inc(scores_ready, 1)

                def products(k, hf):
                    g, t = k // TILES, k % TILES
                    if hf == 0:
                        pe.wait_ge(probs_ready, UNITS * b + GROUP * (k + 1))
                    if t == 0 and (g >= 1 or not first):
                        pe.wait_ge(acc_free, 2 * GROUPS * b + 2 * (g - 1) + hf + 1)
                    for h in range(GROUP):
                        at = (g % 2) * HEAD_DIM
                        ins = mm(bank[ACC + hf][VW * h:VW * (h + 1), :], v[:, t, (g // 2) * GROUP + h, at:at + VW],
                                 probs[:, k % 2, h, hf * HALF:(hf + 1) * HALF], t == 0, t == TILES - 1)
                    ins.then_inc(pv_done, 1)

                for k in range(STEPS):
                    if k == RELOAD and not last:
                        pe.wait_ge(flag_ready, b + 2)
                    score(GROUP * k)
                    if k == RELOAD and not last:
                        pe.reg_load(general, flag[0:1, 0:1])
                    g = k // TILES
                    if k % TILES == PREPARE and not (last and g == GROUPS - 1):
                        nb = b if g < GROUPS - 1 else b + 1
                        prepare_shift(GROUPS * b + g + 1, nb, (g + 1) % GROUPS, freed(b) + before(items, k))
                    do_items(2 * k)
                    score(GROUP * k + 1)
                    if k:
                        products(k - 1, 0)
                    score(GROUP * k + 2)
                    do_items(2 * k + 1)
                    score(GROUP * k + 3)
                    if k:
                        products(k - 1, 1)
                products(STEPS - 1, 0)
                products(STEPS - 1, 1)

                for kind, j in (("v", 0), ("v", 1), ("v", 2), ("out", 0), ("out", 1), ("v", 3), ("out", 2), ("out", 3)):
                    if kind == "out":
                        project(b, CHUNKS - 1, j, bank[j]).then_inc(post_fill, 1)
                    elif not last:
                        do_work(b, items, place(items, kind, j))

            def post(b, last):
                def feed_forward(w_parts):
                    def ready(f):
                        return POST * b + f + 1

                    for what, n in POST_FILLS[AT["gate", 0]:]:
                        f = AT[what, n]
                        o = bank[f % 4]
                        pe.wait_ge(post_free, POST * b + f - 3)
                        if what == "x1T":
                            ins = flip_x1(f, n)
                        elif what in ("gate", "up"):
                            w = gateT if what == "gate" else upT
                            hf, hc = n // HCHUNKS, n % HCHUNKS
                            if what == "gate" and hc == 0:
                                pe.wait_ge(post_free, ready(AT["x1T", 2 * hf + 1]))
                            terms = [(k, i, part) for k in range(CHUNKS) for part in range(w_parts) for i in range(2)]
                            for m, (k, i, part) in enumerate(terms):
                                at = k * HIDDEN + hc * P
                                ins = mm(o, w[:, part, at:at + P], x1T[i][:, k, hf * HALF:(hf + 1) * HALF],
                                         m == 0, m == len(terms) - 1)
                        else:
                            hf = n // 2
                            pe.wait_ge(h_lo_ready, 2 * HCHUNKS * b + HCHUNKS * (hf + 1))
                            for s in range(2):
                                t = (2 * n + s) % TPH
                                terms = [(hc, i, part) for hc in range(HCHUNKS) for part in range(w_parts)
                                         for i in range(2)]
                                for m, (hc, i, part) in enumerate(terms):
                                    ins = mm(o[:, s * DIM:(s + 1) * DIM], hT[hf][i][:, hc, t * P:(t + 1) * P],
                                             downT[:, part, hc * DIM:(hc + 1) * DIM], m == 0, m == len(terms) - 1)
                        ins.then_inc(post_fill, 1)

                def flip_x1(f, n):
                    hf, c = n // 2, n % 2
                    pe.wait_ge(x1_ready, 4 * b + 2 * hf + 2)
                    for i in range(TPH):
                        ins = flip(bank[f % 4][:, i * P:(i + 1) * P], x_res[:, hf * TPH + i, c * P:(c + 1) * P])
                    return ins

                def next_xT(j):
                    if not last:
                        do_work(b, ITEMS, place(ITEMS, "next xT", j))

                next_xT(0)
                next_xT(1)
                for n in range(2):
                    f = AT["x1T", n]
                    pe.wait_ge(post_free, POST * b + f - 3)
                    flip_x1(f, n).then_inc(post_fill, 1)
                next_xT(2)
                next_xT(3)
                with pe.If_eq(wide_weights, 1):
                    feed_forward(3)
                with pe.Else():
                    feed_forward(1)

            for n in range(len(FIRST)):
                do_work(0, FIRST, n)
            pe.wait_ge(flag_ready, 1)
            pe.reg_load(general, flag[0:1, 0:1])
            pe.wait_ge(act_free, FIRST_ACT)
            prepare_shift(0, 0, 0, freed(0))
            pe.wait_ge(wmax_ready, 1)
            for f in range(4, fills):
                flip_weights(f)
            pe.wait_ge(wide_ready, 1)
            pe.reg_load(wide_weights, wide[0:1, 0:1])
            pe.wait_ge(setup_free, fills)

            def batch(b, first, last):
                attention(b, first, last)
                post(b, last)

            batch(0, True, False)
            with pe.Fori(1, BATCHES - 1) as b:
                batch(b, False, False)
            batch(BATCHES - 1, False, True)


_INS = ["L0_attn_x", "L0_attn_Wq", "L0_attn_bq", "L0_attn_Wk", "L0_attn_bk", "L0_attn_Wv", "L0_attn_bv",
        "L0_attn_Wo", "L0_attn_bo", "L0_ffn_w_gate", "L0_ffn_w_up", "L0_ffn_w_down"]


def kernel(**inputs):
    import numpy as _np
    import concourse.bacc as _bacc
    from concourse import mybir as _mybir
    from concourse.bass_utils import run_bass_kernel_spmd as _run

    nc = _bacc.Bacc("TRN2", target_bir_lowering=False, num_devices=1)
    arrays, args = {}, []
    for name in _INS:
        a = _np.ascontiguousarray(inputs[name])
        arrays[f"in_{name}"] = a
        args.append(nc.dram_tensor(f"in_{name}", a.shape, _mybir.dt.from_np(a.dtype), kind="ExternalInput").ap())
    args.append(nc.dram_tensor("out_0", (BATCHES, TOKENS, DIM), _mybir.dt.float32, kind="ExternalOutput").ap())
    build(nc, *args)
    r = _run(nc, [arrays], core_ids=[0])
    return r.results[0]["out_0"]
```
